# Optimizing a Trainium2 kernel written in Bass

```python
import numpy as np
import jax
import jax.numpy as jnp

def _softmax(x, axis=-1):
    return jax.nn.softmax(x, axis=axis)

def _gelu(x):
    return jax.nn.gelu(x, approximate=True)

def _silu(x):
    return jax.nn.silu(x)

def _sigmoid(x):
    return jax.nn.sigmoid(x)

def _layernorm(x, axis=-1, eps=1e-05):
    m = jnp.mean(x, axis=axis, keepdims=True)
    v = jnp.var(x, axis=axis, keepdims=True)
    return (x - m) / jnp.sqrt(v + eps)

def _scatter_add(tgt, idx, src, axis=0):
    return tgt.at[idx].add(src)

def _segment_sum(src, seg, n):
    return jax.ops.segment_sum(src, seg, n)
kernel_name = 'mk_xattn_ffn_d1_seqx_r8_bac557'

def setup_inputs(seed: int=0):
    np.random.seed(seed)
    _w = jnp.asarray

    def _rec_inputs():
        import jax
        import jax.numpy as jnp
        _rk = jax.random.key(seed)
        x = -7.109e-05 + 0.9999 * jax.random.normal(jax.random.fold_in(_rk, 1), (16, 56, 512), jnp.float32)
        _lenS = 56 - jax.random.randint(jax.random.fold_in(_rk, 7), (16,), 0, max(1, 56 // 4) + 1, jnp.int32)
        _lenS2 = 1500 - jax.random.randint(jax.random.fold_in(_rk, 8), (16,), 0, max(1, 1500 // 4) + 1, jnp.int32)
        _ctx_4096P = jax.random.normal(jax.random.fold_in(_rk, 11), (16, 16, 512), jnp.float32)
        _ctx_4096c = jax.random.dirichlet(jax.random.fold_in(_rk, 511), 0.3 * jnp.ones((16,), jnp.float32), (16, 1500))
        _ctx_4096t = jnp.einsum('bsk,bkd->bsd', _ctx_4096c, _ctx_4096P)
        _ctx_4096t = _ctx_4096t * jax.lax.rsqrt(jnp.mean(jnp.square(_ctx_4096t)) + 1e-12) * 0.953939
        ctx_4096 = -2.6191e-05 + 0.999952 * (_ctx_4096t + 0.3 * jax.random.normal(jax.random.fold_in(_rk, 611), (16, 1500, 512), jnp.float32))
        return (x, ctx_4096)
    x, ctx_4096 = _rec_inputs()

    def _L0_xattn_setup():
        import jax, jax.numpy as jnp
        import numpy as np
        TEXT_DIM = 512
        FEATURE_DIM = 512

        def _xavier_uniform(key, shape):
            fan_in, fan_out = (shape[1], shape[0])
            limit = float(np.sqrt(6.0 / (fan_in + fan_out)))
            return jax.random.uniform(key, shape, jnp.float32, -limit, limit)
        key = jax.random.key(seed)
        k1, k2, k3, k4 = jax.random.split(key, 4)
        text = jax.random.normal(k1, (8, 256, TEXT_DIM), jnp.float32)
        features = jax.random.normal(k2, (8, 72, FEATURE_DIM), jnp.float32)
        Wq = _xavier_uniform(k3, (FEATURE_DIM, TEXT_DIM))
        bq = jnp.zeros((FEATURE_DIM,), jnp.float32)
        Wk = _xavier_uniform(k4, (FEATURE_DIM, FEATURE_DIM))
        bk = jnp.zeros((FEATURE_DIM,), jnp.float32)
        return {'text': text, 'features': features, 'Wq': Wq, 'bq': bq, 'Wk': Wk, 'bk': bk}
    _L0_xattn_all = _L0_xattn_setup()
    _L0_xattn_in = {k: v for k, v in _L0_xattn_all.items() if k in ('Wq', 'bq', 'Wk', 'bk')}
    del _L0_xattn_all

    def _L0_ffn_setup():
        import jax, jax.numpy as jnp
        import numpy as np
        H = 512
        I = 256
        E = 16
        TOPK = 4
        SI = 256
        key = jax.random.key(seed)
        ks = jax.random.split(key, 9)
        s = 0.02
        return {'hidden_states': jax.random.normal(ks[0], (2, 256, H), dtype=jnp.float32), 'gate_w': jax.random.normal(ks[1], (E, H), dtype=jnp.float32) * s, 'bias': jnp.zeros((E,), dtype=jnp.float32), 'Wg': jax.random.normal(ks[2], (E, I, H), dtype=jnp.float32) * s, 'Wu': jax.random.normal(ks[3], (E, I, H), dtype=jnp.float32) * s, 'Wd': jax.random.normal(ks[4], (E, H, I), dtype=jnp.float32) * s, 'Sg': jax.random.normal(ks[5], (SI, H), dtype=jnp.float32) * s, 'Su': jax.random.normal(ks[6], (SI, H), dtype=jnp.float32) * s, 'Sd': jax.random.normal(ks[7], (H, SI), dtype=jnp.float32) * s}
    _L0_ffn_all = _L0_ffn_setup()
    _L0_ffn_in = {k: v for k, v in _L0_ffn_all.items() if k in ('gate_w', 'bias', 'Wg', 'Wu', 'Wd', 'Sg', 'Su', 'Sd')}
    del _L0_ffn_all
    return {'x': x, 'ctx_4096': ctx_4096, 'L0_xattn_Wq': _L0_xattn_in['Wq'], 'L0_xattn_bq': _L0_xattn_in['bq'], 'L0_xattn_Wk': _L0_xattn_in['Wk'], 'L0_xattn_bk': _L0_xattn_in['bk'], 'L0_ffn_gate_w': _L0_ffn_in['gate_w'], 'L0_ffn_bias': _L0_ffn_in['bias'], 'L0_ffn_Wg': _L0_ffn_in['Wg'], 'L0_ffn_Wu': _L0_ffn_in['Wu'], 'L0_ffn_Wd': _L0_ffn_in['Wd'], 'L0_ffn_Sg': _L0_ffn_in['Sg'], 'L0_ffn_Su': _L0_ffn_in['Su'], 'L0_ffn_Sd': _L0_ffn_in['Sd']}

def reference(x, ctx_4096, L0_xattn_Wq, L0_xattn_bq, L0_xattn_Wk, L0_xattn_bk, L0_ffn_gate_w, L0_ffn_bias, L0_ffn_Wg, L0_ffn_Wu, L0_ffn_Wd, L0_ffn_Sg, L0_ffn_Su, L0_ffn_Sd):
    import jax
    import jax.numpy as jnp

    def _L0_xattn_ref(text, features, Wq, bq, Wk, bk):
        import jax, jax.numpy as jnp
        import numpy as np
        TEXT_DIM = 512
        FEATURE_DIM = 512

        def _xavier_uniform(key, shape):
            fan_in, fan_out = (shape[1], shape[0])
            limit = float(np.sqrt(6.0 / (fan_in + fan_out)))
            return jax.random.uniform(key, shape, jnp.float32, -limit, limit)
        Q = jnp.einsum('btx,dx->btd', text, Wq) + bq
        K = jnp.einsum('bpx,dx->bpd', features, Wk) + bk
        scale = 1.0 / jnp.sqrt(jnp.asarray(K.shape[-1], K.dtype))
        scores = jnp.einsum('btd,bpd->btp', Q, K) * scale
        attn = jax.nn.softmax(scores, axis=-1)
        attended = jnp.einsum('btp,bpd->btd', attn, features)
        return attended

    def _L0_ffn_ref(hidden_states, gate_w, bias, Wg, Wu, Wd, Sg, Su, Sd):
        import jax, jax.numpy as jnp
        import numpy as np
        H = 512
        I = 256
        E = 16
        TOPK = 4
        SI = 256
        orig_shape = hidden_states.shape
        x = hidden_states.reshape(-1, orig_shape[-1])
        scores = jax.nn.sigmoid(x @ gate_w.T) + bias
        topk_w, topk_idx = jax.lax.top_k(scores, TOPK)
        topk_w = topk_w / (jnp.sum(topk_w, axis=-1, keepdims=True) + 1e-20)
        cw = jnp.sum(jax.nn.one_hot(topk_idx, E, dtype=x.dtype) * topk_w[..., None], axis=1)
        g = jnp.einsum('th,eih->eti', x, Wg)
        u = jnp.einsum('th,eih->eti', x, Wu)
        z = jax.nn.silu(g) * u
        zw = z * cw.T[:, :, None]
        out = jnp.einsum('eti,ehi->th', zw, Wd)
        out = out + jax.nn.silu(x @ Sg.T) * (x @ Su.T) @ Sd.T
        return out.reshape(orig_shape)
    x = x + _L0_xattn_ref(_layernorm(x, axis=-1), ctx_4096, L0_xattn_Wq, L0_xattn_bq, L0_xattn_Wk, L0_xattn_bk)
    x = x + _L0_ffn_ref(_layernorm(x, axis=-1), L0_ffn_gate_w, L0_ffn_bias, L0_ffn_Wg, L0_ffn_Wu, L0_ffn_Wd, L0_ffn_Sg, L0_ffn_Su, L0_ffn_Sd)
    return x

_drawn_inputs = setup_inputs


def setup_inputs(seed=0):
    import zlib

    import numpy as np

    out = dict(_drawn_inputs(seed))
    spreads = {'L0_xattn_bq': (0.0, 0.467), 'L0_xattn_bk': (0.0, 0.8), 'L0_ffn_bias': (0.0, 0.599)}
    factors = {'L0_ffn_gate_w': 4.863, 'L0_ffn_Wg': 3.751, 'L0_ffn_Wu': 3.692, 'L0_ffn_Wd': 3.67}
    for name, (base, spread) in spreads.items():
        noise = np.random.default_rng([zlib.crc32(name.encode()), seed]).standard_normal(out[name].shape)
        drawn = base * np.exp(spread * noise) if base else spread * noise
        out[name] = jnp.asarray(drawn.astype(out[name].dtype))
    for name, factor in factors.items():
        out[name] = (out[name] * factor).astype(out[name].dtype)
    return out
```

```python
import concourse.bass as bass
from concourse import mybir
from contextlib import ExitStack
import numpy as np

BATCH, TEXT, DIM = 16, 56, 512
CTX = 1500
EXPERTS, INNER, TOPK = 16, 256, 4
P = 128
KD = DIM // P
KI = INNER // P
PAIRS = BATCH // 2
HALF = P // 2
PAIR_TOKENS = 2 * TEXT
TOKENS = BATCH * TEXT
ROW_TILE = 125
ROW_TILES = CTX // ROW_TILE
GROUPS = 3
PER_GROUP = ROW_TILES // GROUPS
CHUNKS = 3
CHUNK = CTX // CHUNKS
SPRAY = 112
SCALE = float(DIM) ** -0.5
EPS = 1e-5
REGION = 1024
TILES_MAX = -(-TOKENS // P)
DUMP = EXPERTS * REGION
RING = 8
WFREE = KD * 2 * INNER + KI * DIM

C_ID, C_TRI, C_IOTA, C_REGION = 0, P, 2 * P, 2 * P + EXPERTS
C_VALID = C_REGION + EXPERTS
C_DUMP = C_VALID + 1
C_STEP = C_DUMP + TOPK
C_TOK = C_STEP + 1
C_THR = C_TOK + 1
C_ALL = C_THR + TILES_MAX


class Chain:

    def __init__(self, eng, sem):
        self.eng, self.sem, self.base, self.n = eng, sem, 0, 0

    def mark(self, ins):
        ins.then_inc(self.sem, 1)
        self.n += 1

    def link(self, ins):
        self.mark(ins)
        self.eng.wait_ge(self.sem, self.base + self.n)

    def body(self, start, i, per):
        self.base, self.n = start + i * per, 0

    def now(self):
        return self.base + self.n


def moe_attention_kernel(nc, x, ctx, ctx_t, wq_t, bq, wk, bk, gate_t, gate_b, experts, shared,
                         consts, entry_init, out):
    fp32, bf16 = mybir.dt.float32, mybir.dt.bfloat16
    i32, u32 = mybir.dt.int32, mybir.dt.uint32
    ALU, ACT, AX = mybir.AluOpType, mybir.ActivationFunctionType, mybir.AxisListType

    h_rows = nc.dram_tensor("h_rows", [TOKENS + P, DIM], fp32, kind="Internal").ap()
    entries = nc.dram_tensor("entries", [DUMP + PAIRS * TOPK * P, 2], i32, kind="Internal").ap()

    x_v = x.rearrange("(r b) t d -> b t r d", b=2)
    nat_v = ctx.rearrange("(r b) (p g c) d -> r g p b (c d)", b=2, g=GROUPS, c=PER_GROUP)

    es = ExitStack()
    with es:
        def sb(name, shape, dt=fp32):
            return es.enter_context(nc.sbuf_tensor(name, shape, dt))

        def sem(name):
            return es.enter_context(nc.semaphore(name))

        ctx_cols = sb("ctx_cols", [P, KD * 2 * CTX])
        ctx_rows = sb("ctx_rows", [P, GROUPS, 2, PER_GROUP * DIM])
        xs = sb("xs", [P, PAIRS, DIM])
        wq_sb = sb("wq_sb", [P, KD, DIM])
        wk_sb = sb("wk_sb", [P, KD, DIM])
        shared_sb = sb("shared_sb", [P, WFREE])
        gate_sb = sb("gate_sb", [P, KD, EXPERTS])
        gate_bias = sb("gate_bias", [P, EXPERTS])
        bq_sb = sb("bq_sb", [P, KD])
        bk_sb = sb("bk_sb", [P, KD])
        cst = sb("cst", [P, C_ALL])
        tri = sb("tri", [P, P], bf16)
        ones = sb("ones", [P, P], bf16)
        zero_rows = sb("zero_rows", [P, DIM])
        neg_half = sb("neg_half", [P, 1])
        xn = sb("xn", [P, DIM])
        xn_t = sb("xn_t", [P, KD, P])
        q_t = sb("q_t", [P, KD, P])
        g_t = sb("g_t", [P, KD, P])
        probs = sb("probs", [P, CTX])
        probs_t = sb("probs_t", [P, ROW_TILES * P])
        h = sb("h", [P, DIM])
        h_t = sb("h_t", [P, KD, P])
        acc = sb("acc", [P, DIM])
        expo = sb("expo", [P, KI, P])
        expo1 = sb("expo1", [P, KI, P])
        recip = sb("recip", [P, KI, P])
        gated = sb("gated", [P, KI, P])
        z = sb("z", [P, KI, P])
        stats = sb("stats", [P, 6])
        mean_var = sb("mean_var", [P, 2])
        var_eps = sb("var_eps", [P, 1])
        rstd = sb("rstd", [P, 1])
        row_max = sb("row_max", [P, 1])
        max_c = sb("max_c", [P, 1])
        exp_bias = sb("exp_bias", [P, 1])
        row_sum = sb("row_sum", [P, 1])
        row_inv = sb("row_inv", [P, 1])
        c_sb = sb("c_sb", [P, 1])
        g_exp = sb("g_exp", [P, EXPERTS])
        g_exp1 = sb("g_exp1", [P, EXPERTS])
        g_sig = sb("g_sig", [P, EXPERTS])
        g_score = sb("g_score", [P, EXPERTS])
        top = sb("top", [P, 8])
        top_i = sb("top_i", [P, 8], u32)
        top_f = sb("top_f", [P, TOPK])
        w_sum = sb("w_sum", [P, 1])
        w_inv = sb("w_inv", [P, 1])
        onehot = sb("onehot", [P, TOPK, EXPERTS])
        picked = sb("picked", [P, EXPERTS])
        mask = sb("mask", [P, EXPERTS], bf16)
        base = sb("base", [P, EXPERTS])
        rank = sb("rank", [P, EXPERTS])
        rank_sel = sb("rank_sel", [P, TOPK, EXPERTS])
        place_f = sb("place_f", [P, TOPK])
        place = sb("place", [P, TOPK], i32)
        dump_at = sb("dump_at", [P, TOPK])
        token = sb("token", [P, 1])
        entry = sb("entry", [P, TOPK, 2], i32)
        cnt = sb("cnt", [1, EXPERTS])
        above = sb("above", [1, EXPERTS, TILES_MAX])
        n_tiles = sb("n_tiles", [1, EXPERTS])
        active = sb("active", [1, EXPERTS])
        incl = sb("incl", [1, EXPERTS])
        excl = sb("excl", [1, EXPERTS])
        turn = sb("turn", [1, EXPERTS, EXPERTS])
        turn_on = sb("turn_on", [1, EXPERTS, EXPERTS])
        turn_n = sb("turn_n", [1, EXPERTS, EXPERTS])
        turn_e = sb("turn_e", [1, EXPERTS, EXPERTS])
        plan_f = sb("plan_f", [1, 2 * EXPERTS + 2])
        plan = sb("plan", [1, 2 * EXPERTS + 2], i32)
        ring = sb("ring", [P, RING, 2], i32)
        take_at = sb("take_at", [P, 1], i32)
        add_at = sb("add_at", [P, 1], i32)
        taken = sb("taken", [P, DIM])
        taken_t = sb("taken_t", [P, KD, P])
        y_sb = sb("y_sb", [P, DIM])

        ident = cst[:, C_ID:C_ID + P]
        iota16 = cst[:, C_IOTA:C_IOTA + EXPERTS]
        region = cst[:, C_REGION:C_REGION + EXPERTS]
        valid = cst[:, C_VALID:C_VALID + 1]

        scores = es.enter_context(nc.psum_tensor("scores", [P, CHUNKS, 512], fp32))
        b3, b4, b5, b6, b7 = (es.enter_context(nc.psum_tensor(n, [P, 512], fp32))
                              for n in ("b3", "b4", "b5", "b6", "b7"))

        x_loaded, c_loaded = sem("x_loaded"), sem("c_loaded")
        wq_loaded, wk_loaded, sh_loaded = sem("wq_loaded"), sem("wk_loaded"), sem("sh_loaded")
        cols_loaded = [sem(f"cols_loaded{k}") for k in range(KD)]
        rows_loaded = [sem(f"rows_loaded{g}") for g in range(GROUPS)]
        cols_used, rows_used = sem("cols_used"), sem("rows_used")
        init_ready, init_stored = sem("init_ready"), sem("init_stored")
        var_ready, rstd_ready, xn_ready = sem("var_ready"), sem("rstd_ready"), sem("xn_ready")
        xt_ready, xnt_ready = sem("xt_ready"), sem("xnt_ready")
        q_ready, qt_ready, g_ready, gt_ready, c_read = (sem("q_ready"), sem("qt_ready"), sem("g_ready"),
                                                       sem("gt_ready"), sem("c_read"))
        scores_ready, bias_ready, probs_ready = sem("scores_ready"), sem("bias_ready"), sem("probs_ready")
        pt_ready, ptt_ready, attended_ready = sem("pt_ready"), sem("ptt_ready"), sem("attended_ready")
        x1_ready, h_ready, ht_ready, htt_ready = sem("x1_ready"), sem("h_ready"), sem("ht_ready"), sem("htt_ready")
        gate_ready, gexp_ready, mask_ready = sem("gate_ready"), sem("gexp_ready"), sem("mask_ready")
        rank_ready, rank_read, entries_ready = sem("rank_ready"), sem("rank_read"), sem("entries_ready")
        entries_stored, h_stored, acc_stored = sem("entries_stored"), sem("h_stored"), sem("acc_stored")
        up_ready, expo_ready, z_ready, y_ready, acc_ready = (sem("up_ready"), sem("expo_ready"), sem("z_ready"),
                                                             sem("y_ready"), sem("acc_ready"))
        plan_ready, entry_loaded, entry_free = sem("plan_ready"), sem("entry_loaded"), sem("entry_free")
        expert_loaded = [sem(f"expert_loaded{i}") for i in range(2)]
        expert_used = [sem(f"expert_used{i}") for i in range(2)]
        gathered, taken_used, tt_ready = sem("gathered"), sem("taken_used"), sem("tt_ready")
        ysb_ready, added = sem("ysb_ready"), sem("added")
        waited = sem("waited")
        dve_step, pool_step = sem("dve_step"), sem("pool_step")

        block = es.enter_context(nc.Block())

        def settle(eng):
            eng.sem_inc(waited, 1)

        expert_w = [ctx_cols[:, i * WFREE:(i + 1) * WFREE] for i in range(2)]

        @block.sync
        def _(sp):
            sp.sem_inc(entry_loaded, 16)
            sp.dma_start(cst[:], consts).then_inc(c_loaded, 16)
            for b in range(2):
                sp.dma_start(xs[HALF * b:HALF * b + TEXT, :, :], x_v[b]).then_inc(x_loaded, 16)
            for b in range(2):
                sp.dma_start(xs[HALF * b + TEXT:HALF * (b + 1), :, :], entry_init[1]).then_inc(x_loaded, 16)
            sp.dma_start(wq_sb[:], wq_t).then_inc(wq_loaded, 16)
            sp.dma_start(bq_sb[:], bq).then_inc(wq_loaded, 16)
            sp.dma_start(wk_sb[:], wk).then_inc(wk_loaded, 16)
            sp.dma_start(bk_sb[:], bk).then_inc(wk_loaded, 16)

            def load_cols(r, k):
                sp.dma_start(ctx_cols[:, k * 2 * CTX:(k + 1) * 2 * CTX],
                             ctx_t[bass.ds(r, 1), k, :, :].rearrange("a p n -> (a p) n")).then_inc(cols_loaded[k], 16)

            def load_rows(r, g):
                v = nat_v[bass.ds(r, 1), g, :, :, :].rearrange("a p b n -> (a p) b n")
                sp.dma_start(ctx_rows[0:SPRAY, g, :, :], v[0:SPRAY]).then_inc(rows_loaded[g], 16)
                sp.dma_start(ctx_rows[SPRAY:ROW_TILE, g, :, :], v[SPRAY:ROW_TILE]).then_inc(rows_loaded[g], 16)

            for k in range(KD):
                load_cols(0, k)
            for g in range(GROUPS):
                load_rows(0, g)
            sp.dma_start(gate_sb[:], gate_t).then_inc(sh_loaded, 16)
            sp.dma_start(gate_bias[:], gate_b.to_broadcast([P, EXPERTS])).then_inc(sh_loaded, 16)
            sp.dma_start(shared_sb[:], shared).then_inc(sh_loaded, 16)
            sp.wait_ge(init_ready, 1)
            sp.dma_start(h_rows[TOKENS:TOKENS + P, :], zero_rows[:]).then_inc(init_stored, 16)

            with sp.Fori(0, PAIRS - 1) as r:
                for k in range(KD):
                    sp.wait_ge(cols_used, r * KD + (k + 1))
                    load_cols(r + 1, k)
                for g in range(GROUPS):
                    sp.wait_ge(rows_used, r * GROUPS + (g + 1))
                    load_rows(r + 1, g)

            sp.wait_ge(cols_used, KD * PAIRS)
            sp.wait_ge(plan_ready, 1)
            sp.wait_ge(entries_stored, (PAIRS * TOPK + 1) * 16)
            t = sp.alloc_register("sp_tile")
            sp.reg_mov(t, 0)
            with sp.Fori(0, EXPERTS // 2) as turn2:
                for s in range(2):
                    n = sp.value_load(plan[0:1, bass.ds(turn2 * 2 + s, 1)], min_val=0, max_val=TILES_MAX)
                    e = sp.value_load(plan[0:1, bass.ds(turn2 * 2 + (EXPERTS + s), 1)], min_val=0, max_val=EXPERTS - 1)
                    with sp.If(n > 0):
                        sp.wait_ge(expert_used[s], turn2 + 1)
                        sp.dma_start(expert_w[s], experts[bass.ds(e, 1), :, :].rearrange("a p n -> (a p) n")
                                     ).then_inc(expert_loaded[s], 16)
                        settle(sp)
                        with sp.Fori(0, n) as j:
                            tv = sp.snap(t, min_val=0, max_val=EXPERTS * TILES_MAX)
                            free, loaded = sp.snap(tv + 1), sp.snap((tv + 1) * 16)
                            slot, at = sp.snap(tv % RING), sp.snap((e * (REGION // P) + j) * P)
                            sp.wait_ge(entry_free, free)
                            settle(sp)
                            sp.wait_ge(entry_loaded, loaded)
                            settle(sp)
                            sp.dma_start(ring[:, bass.ds(slot, 1), :].rearrange("p a c -> p (a c)"),
                                         entries[bass.ds(at, P), :]
                                         ).then_inc(entry_loaded, 16)
                            sp.reg_add(t, t, 1)

        @block.gpsimd
        def _(pool):
            nc.gpsimd.memset(neg_half[:], -0.5).then_inc(pool_step, 1)
            nc.gpsimd.memset(zero_rows[:], 0.0).then_inc(init_ready, 1)
            pool.sem_inc(entry_free, RING)
            pool.wait_ge(pool_step, 1)

            pool.wait_ge(init_ready, 1)
            pool.dma_start(entries[0:DUMP, :].rearrange("(p n) c -> p (n c)", p=P), entry_init[0]
                           ).then_inc(entries_stored, 16)
            pool.dma_start(out[TOKENS:TOKENS + P, :], zero_rows[:]).then_inc(added, 16)

            def power(i):
                pool.wait_ge(var_ready, i + 1)
                nc.gpsimd.tensor_tensor(rstd[:], var_eps[:], neg_half[:], ALU.pow).then_inc(rstd_ready, 1)

            def scatter(r):
                pool.wait_ge(entries_ready, r + 1)
                settle(pool)
                for k in range(TOPK):
                    nc.gpsimd.indirect_dma_start(
                        entries[:, :], bass.IndirectOffsetOnAxis(ap=place[:, k:k + 1], axis=0),
                        entry[:, k, :], None).then_inc(entries_stored, 16)

            power(0)
            power(1)
            pool.wait_ge(entries_stored, 16)
            with pool.Fori(1, PAIRS - 1) as p:
                power(p * 2)
                power(p * 2 + 1)
                scatter(p - 1)
            power(2 * PAIRS - 2)
            scatter(PAIRS - 2)
            power(2 * PAIRS - 1)
            scatter(PAIRS - 1)

            pool.wait_ge(plan_ready, 1)
            lead = pool.value_load(plan[0:1, 2 * EXPERTS + 1:2 * EXPERTS + 2], min_val=TOKENS * TOPK // P - 2,
                                   max_val=TOKENS * TOPK // P + EXPERTS)
            pool.wait_ge(init_stored, 16)
            pool.wait_ge(h_stored, PAIRS * 32 + 16)
            pool.wait_ge(acc_stored, PAIRS * 32 + 16)

            def gather(t):
                pool.wait_ge(entry_loaded, (t + 2) * 16)
                nc.gpsimd.tensor_copy(take_at[:], ring[:, bass.ds(t % RING, 1), 0]).then_inc(pool_step, 1)

            def gather_start(t):
                pool.wait_ge(taken_used, t)
                settle(pool)
                nc.gpsimd.indirect_dma_start(taken[:], None, h_rows[:, :],
                                             bass.IndirectOffsetOnAxis(ap=take_at[:, 0:1], axis=0)
                                             ).then_inc(gathered, 16)

            def add(t):
                pool.wait_ge(added, (t + 1) * 16)
                settle(pool)
                nc.gpsimd.indirect_dma_start(out[:, :], bass.IndirectOffsetOnAxis(ap=add_at[:, 0:1], axis=0),
                                             y_sb[:], None, compute_op=ALU.add).then_inc(added, 16)

            def add_index(t):
                nc.gpsimd.tensor_copy(add_at[:], ring[:, bass.ds(t % RING, 1), 0]).then_inc(entry_free, 1)

            def take(t):
                pool.wait_ge(gathered, t * 16)
                gather(t)
                pool.wait_ge(pool_step, t + 2)
                gather_start(t)

            def give(t):
                pool.wait_ge(added, (t + 1) * 16)
                pool.wait_ge(ysb_ready, t + 2)
                add_index(t)
                pool.wait_ge(entry_free, t + (RING + 1))
                add(t)

            take(0)
            take(1)
            with pool.Fori(0, lead) as t:
                take(t + 2)
                give(t)
            pool.wait_ge(gathered, (lead + 2) * 16)
            gather_start(lead + 2)
            give(lead)
            give(lead + 1)
            pool.wait_ge(added, (lead + 3) * 16)
            pool.wait_ge(gathered, (lead + 3) * 16)

        @block.tensor
        def _(pe):
            def transposes(bank, src):
                for k in range(KD):
                    last = nc.tensor.transpose(bank[:, k * P:(k + 1) * P], src[:, k * P:(k + 1) * P], ident)
                return last

            def x_transpose(p, bank):
                pe.wait_ge(xn_ready, p + 1)
                transposes(bank, xn).then_inc(xt_ready, 1)

            def project(p):
                pe.wait_ge(xnt_ready, p + 1)
                for m in range(KD):
                    for k in range(KD):
                        last = nc.tensor.matmul(b6[:, m * P:(m + 1) * P], wq_sb[:, k, m * P:(m + 1) * P],
                                                xn_t[:, k, :], start=(k == 0), stop=(k == KD - 1))
                last.then_inc(q_ready, 1)
                pe.wait_ge(qt_ready, p + 1)
                for m in range(KD):
                    for k in range(KD):
                        last = nc.tensor.matmul(b7[:, m * P:(m + 1) * P], wk_sb[:, k, m * P:(m + 1) * P],
                                                q_t[:, k, :], start=(k == 0), stop=(k == KD - 1))
                last.then_inc(g_ready, 1)

            def project_bias(p):
                for k in range(KD):
                    last = nc.tensor.matmul(b3[:, 32:33], q_t[:, k, :], bk_sb[:, k:k + 1],
                                            start=(k == 0), stop=(k == KD - 1))
                last.then_inc(g_ready, 1)

            def score(p):
                pe.wait_ge(gt_ready, p + 1)
                pe.wait_ge(probs_ready, p)
                for k in range(KD):
                    pe.wait_ge(cols_loaded[k], (p + 1) * 16)
                    for n in range(CHUNKS):
                        for b in range(2):
                            at = (2 * k + b) * CTX + n * CHUNK
                            last = nc.tensor.matmul(scores[HALF * b:HALF * (b + 1), n, 0:CHUNK],
                                                    g_t[:, k, HALF * b:HALF * (b + 1)],
                                                    ctx_cols[:, at:at + CHUNK],
                                                    start=(k == 0), stop=(k == KD - 1))
                    last.then_inc(cols_used, 1)

            def attend(p):
                pe.wait_ge(probs_ready, p + 1)
                for g in range(GROUPS):
                    bank = (b4, b5)[g % 2]
                    if g == 1:
                        pe.wait_ge(rank_read, p)
                    if g == 2:
                        pe.wait_ge(ptt_ready, p * GROUPS + 1)
                    for c in range(PER_GROUP):
                        at = (g * PER_GROUP + c) * ROW_TILE
                        last = nc.tensor.transpose(bank[0:ROW_TILE, c * P:(c + 1) * P],
                                                   probs[:, at:at + ROW_TILE], ident)
                    last.then_inc(pt_ready, 1)
                for g in range(GROUPS):
                    pe.wait_ge(ptt_ready, p * GROUPS + (g + 1))
                    pe.wait_ge(rows_loaded[g], (p + 1) * 32)
                    for c in range(PER_GROUP):
                        for b in range(2):
                            at = (g * PER_GROUP + c) * P + HALF * b
                            first, end = g + c == 0, g * PER_GROUP + c == ROW_TILES - 1
                            last = nc.tensor.matmul(b3[HALF * b:HALF * (b + 1), :],
                                                    probs_t[0:ROW_TILE, at:at + HALF],
                                                    ctx_rows[0:ROW_TILE, g, b, c * DIM:(c + 1) * DIM],
                                                    start=first, stop=end)
                    last.then_inc(rows_used, 1)

            def h_transpose(r):
                pe.wait_ge(h_ready, r + 1)
                transposes(b4, h).then_inc(ht_ready, 1)

            def gate(r):
                pe.wait_ge(htt_ready, r + 1)
                for k in range(KD):
                    last = nc.tensor.matmul(b3[:, 0:EXPERTS], h_t[:, k, :], gate_sb[:, k, :],
                                            start=(k == 0), stop=(k == KD - 1))
                last.then_inc(gate_ready, 1)

            def ranks(r):
                pe.wait_ge(mask_ready, r + 1)
                nc.tensor.matmul(b5[:, 0:EXPERTS], tri[:], mask[:], start=True, stop=True)
                nc.tensor.matmul(b5[:, EXPERTS:2 * EXPERTS], ones[:], mask[:], start=True, stop=True
                                 ).then_inc(rank_ready, 1)

            def up(w, src_t):
                for i in range(KI):
                    bank = (b6, b7)[i]
                    for half in range(2):
                        for k in range(KD):
                            at = (2 * k + half) * INNER + i * P
                            last = nc.tensor.matmul(bank[:, half * P:(half + 1) * P], w[:, at:at + P],
                                                    src_t[:, k, :], start=(k == 0), stop=(k == KD - 1))
                    last.then_inc(up_ready, 1)

            def down(w, uses):
                for i in range(KI):
                    pe.wait_ge(z_ready, uses * KI + (i + 1))
                    at = KD * 2 * INNER + i * DIM
                    last = nc.tensor.matmul(b3[:, :], z[:, i, :], w[:, at:at + DIM],
                                            start=(i == 0), stop=(i == KI - 1))
                last.then_inc(y_ready, 1)

            def shared_expert(r):
                up(shared_sb, h_t)
                down(shared_sb, r)

            for s in range(2):
                pe.sem_inc(expert_used[s], 1)
            pe.sem_inc(ht_ready, 1)
            pe.wait_ge(c_loaded, 16)
            x_transpose(0, b5)
            pe.wait_ge(wq_loaded, 32)
            pe.wait_ge(wk_loaded, 32)
            project(0)
            project_bias(0)
            score(0)
            x_transpose(1, b5)
            pe.wait_ge(gt_ready, 1)
            project(1)
            pe.wait_ge(c_read, 1)
            project_bias(1)
            pe.wait_ge(sh_loaded, 48)
            pe.wait_ge(c_read, 2)
            attend(0)
            with pe.Fori(1, PAIRS - 1) as p:
                score(p)
                h_transpose(p - 1)
                x_transpose(p + 1, b5)
                gate(p - 1)
                project(p + 1)
                pe.wait_ge(gexp_ready, p)
                project_bias(p + 1)
                ranks(p - 1)
                pe.wait_ge(gt_ready, p + 2)
                pe.wait_ge(c_read, p + 2)
                shared_expert(p - 1)
                pe.wait_ge(acc_ready, p)
                attend(p)
            last_pair = PAIRS - 1
            score(last_pair)
            h_transpose(last_pair - 1)
            gate(last_pair - 1)
            ranks(last_pair - 1)
            pe.wait_ge(gexp_ready, last_pair)
            attend(last_pair)
            up(shared_sb, h_t)
            pe.wait_ge(x1_ready, PAIRS)
            down(shared_sb, last_pair - 1)
            h_transpose(last_pair)
            pe.wait_ge(acc_ready, last_pair)
            gate(last_pair)
            ranks(last_pair)
            pe.wait_ge(gexp_ready, PAIRS)
            shared_expert(last_pair)

            def tile_transpose(t):
                pe.wait_ge(gathered, (t + 1) * 16)
                transposes(b4, taken).then_inc(taken_used, 1)

            pe.wait_ge(plan_ready, 1)
            t = pe.alloc_register("pe_tile")
            pe.reg_mov(t, 0)
            tile_transpose(0)
            with pe.Fori(0, EXPERTS // 2) as turn2:
                for s in range(2):
                    n = pe.value_load(plan[0:1, bass.ds(turn2 * 2 + s, 1)], min_val=0, max_val=TILES_MAX)
                    with pe.If(n > 0):
                        pe.wait_ge(expert_loaded[s], (turn2 + 1) * 16)
                        settle(pe)
                        with pe.Fori(0, n) as j:
                            tv = pe.snap(t, min_val=0, max_val=EXPERTS * TILES_MAX)
                            pe.wait_ge(tt_ready, tv + 1)
                            up(expert_w[s], taken_t)
                            tile_transpose(tv + 1)
                            pe.wait_ge(acc_ready, PAIRS)
                            pe.wait_ge(ysb_ready, tv + 1)
                            down(expert_w[s], tv + PAIRS)
                            pe.reg_add(t, t, 1)
                        pe.wait_ge(y_ready, pe.snap(t, min_val=0, max_val=EXPERTS * TILES_MAX) + PAIRS)
                        pe.sem_inc(expert_used[s], 1)

        @block.scalar
        def _(act):
            def copy_x_t(p, bank):
                act.wait_ge(xt_ready, p + 1)
                nc.scalar.copy(xn_t[:].rearrange("p k n -> p (k n)"), bank[:, :]).then_inc(xnt_ready, 1)

            def copy_g_t(p):
                act.wait_ge(g_ready, 2 * p + 1)
                nc.scalar.copy(g_t[:].rearrange("p k n -> p (k n)"), b7[:, :]).then_inc(gt_ready, 1)

            def softmax(p):
                act.wait_ge(bias_ready, p + 1)
                nc.scalar.activation(probs[:].rearrange("p (n c) -> p n c", n=CHUNKS), scores[:, :, 0:CHUNK],
                                     ACT.Exp, bias=exp_bias[:], scale=SCALE, accum_out=row_sum[:]
                                     ).then_inc(probs_ready, 1)

            def copy_probs_t(p):
                for g in range(GROUPS):
                    act.wait_ge(pt_ready, p * GROUPS + (g + 1))
                    nc.scalar.copy(probs_t[0:ROW_TILE, g * PER_GROUP * P:(g + 1) * PER_GROUP * P],
                                   (b4, b5)[g % 2][0:ROW_TILE, :]).then_inc(ptt_ready, 1)

            def copy_h_t(r):
                act.wait_ge(ht_ready, r + 2)
                nc.scalar.copy(h_t[:].rearrange("p k n -> p (k n)"), b4[:, :]).then_inc(htt_ready, 1)

            def store_pair(r, src, dst, done):
                for b in range(2):
                    act.dma_start(dst[bass.ds(r * PAIR_TOKENS + b * TEXT, TEXT), :],
                                  src[HALF * b:HALF * b + TEXT, :]).then_inc(done, 16)

            def gate_exp(r):
                act.wait_ge(gate_ready, r + 1)
                nc.scalar.activation(g_exp[:], b3[:, 0:EXPERTS], ACT.Exp, scale=-1.0).then_inc(gexp_ready, 1)

            def up_exp(uses):
                for i in range(KI):
                    act.wait_ge(up_ready, uses * KI + (i + 1))
                    nc.scalar.activation(expo[:, i, :], (b6, b7)[i][:, 0:P], ACT.Exp, scale=-1.0
                                         ).then_inc(expo_ready, 1)

            for done, n in ((h_stored, 16), (acc_stored, 16), (ysb_ready, 1)):
                act.sem_inc(done, n)
            copy_x_t(0, b5)
            copy_g_t(0)
            copy_x_t(1, b5)
            softmax(0)
            copy_g_t(1)
            copy_probs_t(0)
            with act.Fori(1, PAIRS - 1) as p:
                act.wait_ge(h_ready, p)
                store_pair(p - 1, h, h_rows, h_stored)
                copy_h_t(p - 1)
                copy_x_t(p + 1, b5)
                gate_exp(p - 1)
                softmax(p)
                copy_g_t(p + 1)
                up_exp(p - 1)
                copy_probs_t(p)
                act.wait_ge(acc_ready, p)
                store_pair(p - 1, acc, out, acc_stored)
            last_pair = PAIRS - 1
            act.wait_ge(h_ready, last_pair)
            store_pair(last_pair - 1, h, h_rows, h_stored)
            copy_h_t(last_pair - 1)
            gate_exp(last_pair - 1)
            softmax(last_pair)
            copy_probs_t(last_pair)
            up_exp(last_pair - 1)
            act.wait_ge(h_ready, PAIRS)
            store_pair(last_pair, h, h_rows, h_stored)
            copy_h_t(last_pair)
            act.wait_ge(acc_ready, last_pair)
            store_pair(last_pair - 1, acc, out, acc_stored)
            gate_exp(last_pair)
            up_exp(last_pair)
            act.wait_ge(acc_ready, PAIRS)
            store_pair(last_pair, acc, out, acc_stored)

            act.wait_ge(plan_ready, 1)
            total = act.value_load(plan[0:1, 2 * EXPERTS:2 * EXPERTS + 1], min_val=TOKENS * TOPK // P,
                                   max_val=TOKENS * TOPK // P + EXPERTS)

            def copy_taken_t(t):
                act.wait_ge(taken_used, t + 1)
                nc.scalar.copy(taken_t[:].rearrange("p k n -> p (k n)"), b4[:, :]).then_inc(tt_ready, 1)

            copy_taken_t(0)
            with act.Fori(0, total) as t:
                up_exp(t + PAIRS)
                copy_taken_t(t + 1)
                act.wait_ge(y_ready, t + (PAIRS + 1))
                act.wait_ge(added, (t + 1) * 16)
                act.wait_ge(entry_loaded, (t + 2) * 16)
                nc.scalar.activation(y_sb[:], b3[:, :], ACT.Copy,
                                     scale=ring[:, bass.ds(t % RING, 1), 1].bitcast(fp32)).then_inc(ysb_ready, 1)

        @block.vector
        def _(dve):
            ch = Chain(dve, dve_step)

            def normalise(i, src, dst, done):
                settle(dve)
                ch.link(nc.vector.bn_stats(stats[:], src))
                settle(dve)
                ch.link(nc.vector.bn_aggr(mean_var[:], stats[:]))
                nc.vector.tensor_scalar_add(var_eps[:], mean_var[:, 1:2], EPS).then_inc(var_ready, 1)
                dve.wait_ge(rstd_ready, i + 1)
                nc.vector.tensor_scalar(dst[:], src, mean_var[:, 0:1], rstd[:], ALU.subtract, ALU.mult
                                        ).then_inc(done, 1)

            def pair_x(p):
                return xs[:, bass.ds(p, 1), :].rearrange("p a n -> p (a n)")

            def norm_x(p, i):
                if not isinstance(p, int) or p > 0:
                    dve.wait_ge(xt_ready, p)
                normalise(i, pair_x(p), xn, xn_ready)

            def finish_attention(r, i):
                dve.wait_ge(probs_ready, r + 1)
                ch.link(nc.vector.reciprocal(row_inv[:], row_sum[:]))
                dve.wait_ge(rows_used, (r + 1) * GROUPS)
                nc.vector.scalar_tensor_tensor(pair_x(r), b3[:, :], row_inv[:], pair_x(r), ALU.mult, ALU.add
                                               ).then_inc(x1_ready, 1)
                dve.wait_ge(x1_ready, r + 1)
                dve.wait_ge(h_stored, r * 32 + 16)
                dve.wait_ge(ht_ready, r + 1)
                normalise(i, pair_x(r), h, h_ready)

            def score_max(p):
                dve.wait_ge(cols_used, (p + 1) * KD)
                ch.link(nc.vector.reduce_max(row_max[:], scores[:, :, 0:CHUNK], axis=AX.XY))
                dve.wait_ge(c_read, p + 1)
                ch.link(nc.vector.tensor_scalar(max_c[:], row_max[:], c_sb[:], -SCALE, ALU.add, ALU.mult))
                nc.vector.scalar_tensor_tensor(exp_bias[:], c_sb[:], SCALE, max_c[:], ALU.mult, ALU.add
                                               ).then_inc(bias_ready, 1)

            def add_q_bias(p):
                dve.wait_ge(q_ready, p + 1)
                nc.vector.tensor_tensor(q_t[:], b6[:, :].rearrange("p (k n) -> p k n", k=KD),
                                        bq_sb[:].unsqueeze(2).to_broadcast([P, KD, P]), ALU.add
                                        ).then_inc(qt_ready, 1)

            def read_c(p):
                dve.wait_ge(g_ready, 2 * p + 2)
                dve.wait_ge(bias_ready, p)
                nc.vector.tensor_copy(c_sb[:], b3[:, 32:33]).then_inc(c_read, 1)

            def route(r):
                dve.wait_ge(gexp_ready, r + 1)
                ch.link(nc.vector.tensor_scalar_add(g_exp1[:], g_exp[:], 1.0))
                ch.link(nc.vector.reciprocal(g_sig[:], g_exp1[:]))
                ch.link(nc.vector.tensor_tensor(g_score[:], g_sig[:], gate_bias[:], ALU.add))
                settle(dve)
                ch.link(nc.vector.max(top[:], g_score[:]))
                settle(dve)
                ch.link(nc.vector.max_index(top_i[:], top[:], g_score[:]))
                ch.mark(nc.vector.reduce_sum(w_sum[:], top[:, 0:TOPK], axis=AX.X))
                ch.link(nc.vector.tensor_copy(top_f[:], top_i[:, 0:TOPK]))
                ch.link(nc.vector.tensor_tensor(onehot[:], iota16.unsqueeze(1).to_broadcast([P, TOPK, EXPERTS]),
                                                top_f[:].unsqueeze(2).to_broadcast([P, TOPK, EXPERTS]),
                                                ALU.is_equal))
                ch.link(nc.vector.reduce_sum(picked[:], onehot[:].rearrange("p k e -> p e k"), axis=AX.X))
                nc.vector.tensor_scalar(mask[:], picked[:], valid, None, ALU.mult).then_inc(mask_ready, 1)
                ch.link(nc.vector.tensor_scalar_add(w_inv[:], w_sum[:], 1e-20))
                ch.link(nc.vector.reciprocal(w_sum[:], w_inv[:]))
                dve.wait_ge(entries_stored, r * (TOPK * 16) + 16)
                nc.vector.tensor_scalar(entry[:, :, 1].bitcast(fp32), top[:, 0:TOPK], w_sum[:], None, ALU.mult)

            def enter(r):
                dve.wait_ge(rank_ready, r + 1)
                nc.vector.tensor_tensor(rank[:], b5[:, 0:EXPERTS], base[:], ALU.add)
                ch.mark(nc.vector.tensor_tensor(base[:], b5[:, EXPERTS:2 * EXPERTS], base[:], ALU.add))
                ch.link(nc.vector.tensor_copy(entry[:, :, 0], token[:].to_broadcast([P, TOPK])))
                ch.link(nc.vector.tensor_tensor(rank_sel[:], onehot[:],
                                                rank[:].unsqueeze(1).to_broadcast([P, TOPK, EXPERTS]), ALU.mult))
                ch.link(nc.vector.reduce_sum(place_f[:], rank_sel[:], axis=AX.X))
                nc.vector.scalar_tensor_tensor(place[:], place_f[:], valid, dump_at[:], ALU.mult, ALU.add
                                               ).then_inc(entries_ready, 1)
                nc.vector.tensor_scalar(dump_at[:], dump_at[:], cst[:, C_STEP:C_STEP + 1], None, ALU.add)
                nc.vector.tensor_scalar_add(token[:], token[:], float(PAIR_TOKENS)).then_inc(rank_read, 1)

            def silu_times_up(uses):
                for i in range(KI):
                    bank = (b6, b7)[i]
                    dve.wait_ge(expo_ready, uses * KI + (i + 1))
                    ch.link(nc.vector.tensor_scalar_add(expo1[:, i, :], expo[:, i, :], 1.0))
                    ch.link(nc.vector.reciprocal(recip[:, i, :], expo1[:, i, :]))
                    ch.link(nc.vector.tensor_tensor(gated[:, i, :], bank[:, 0:P], recip[:, i, :], ALU.mult))
                    nc.vector.tensor_tensor(z[:, i, :], bank[:, P:2 * P], gated[:, i, :], ALU.mult
                                            ).then_inc(z_ready, 1)

            def add_shared(r):
                dve.wait_ge(y_ready, r + 1)
                dve.wait_ge(acc_stored, r * 32 + 16)
                nc.vector.tensor_tensor(acc[:], b3[:, :], pair_x(r), ALU.add).then_inc(acc_ready, 1)

            dve.wait_ge(c_loaded, 16)
            nc.vector.tensor_copy(tri[:], cst[:, C_TRI:C_TRI + P])
            nc.vector.memset(ones[:], 1.0)
            nc.vector.tensor_copy(base[:], region)
            nc.vector.tensor_copy(dump_at[:], cst[:, C_DUMP:C_DUMP + TOPK])
            ch.link(nc.vector.tensor_copy(token[:], cst[:, C_TOK:C_TOK + 1]))
            dve.wait_ge(x_loaded, 64)
            dve.wait_ge(wq_loaded, 32)
            norm_x(0, 0)
            add_q_bias(0)
            read_c(0)
            norm_x(1, 1)
            score_max(0)
            add_q_bias(1)
            read_c(1)
            dve.wait_ge(sh_loaded, 48)

            def body(p):
                finish_attention(p - 1, p * 2)
                if not isinstance(p, int):
                    norm_x(p + 1, p * 2 + 1)
                score_max(p)
                route(p - 1)
                if not isinstance(p, int):
                    add_q_bias(p + 1)
                    read_c(p + 1)
                enter(p - 1)

            start, per = ch.now(), 28
            with dve.Fori(1, PAIRS - 1) as p:
                ch.body(start, p - 1, per)
                body(p)
                silu_times_up(p - 1)
                add_shared(p - 1)
                assert ch.n == per, ch.n
            last_pair = PAIRS - 1
            ch.base, ch.n = start + (PAIRS - 2) * per, 0
            body(last_pair)
            finish_attention(last_pair, 2 * PAIRS - 1)
            silu_times_up(last_pair - 1)
            add_shared(last_pair - 1)
            route(last_pair)
            enter(last_pair)

            dve.wait_ge(rank_read, PAIRS)
            ch.link(nc.vector.tensor_tensor(cnt[:], base[0:1, :], region[0:1, :], ALU.subtract))
            ch.link(nc.vector.tensor_tensor(above[:], cnt[:].unsqueeze(2).to_broadcast([1, EXPERTS, TILES_MAX]),
                                            cst[0:1, C_THR:C_ALL].unsqueeze(1).to_broadcast([1, EXPERTS, TILES_MAX]),
                                            ALU.is_gt))
            ch.link(nc.vector.reduce_sum(n_tiles[:], above[:], axis=AX.X))
            ch.mark(nc.vector.reduce_sum(plan_f[0:1, 2 * EXPERTS:2 * EXPERTS + 1], n_tiles[:], axis=AX.X))
            ch.link(nc.vector.tensor_scalar_min(active[:], n_tiles[:], 1.0))
            ch.link(nc.vector.tensor_tensor_scan(incl[:], cst[0:1, C_ID:C_ID + 1].to_broadcast([1, EXPERTS]),
                                                 active[:], 0.0, ALU.mult, ALU.add))
            ch.link(nc.vector.tensor_tensor(excl[:], incl[:], active[:], ALU.subtract))
            wide = [1, EXPERTS, EXPERTS]
            ch.link(nc.vector.tensor_tensor(turn[:], excl[:].unsqueeze(1).to_broadcast(wide),
                                            iota16[0:1, :].unsqueeze(2).to_broadcast(wide), ALU.is_equal))
            ch.link(nc.vector.tensor_tensor(turn_on[:], turn[:], active[:].unsqueeze(1).to_broadcast(wide), ALU.mult))
            ch.mark(nc.vector.tensor_tensor(turn_n[:], turn_on[:], n_tiles[:].unsqueeze(1).to_broadcast(wide), ALU.mult))
            ch.link(nc.vector.tensor_tensor(turn_e[:], turn_on[:], iota16[0:1, :].unsqueeze(1).to_broadcast(wide),
                                            ALU.mult))
            ch.mark(nc.vector.tensor_scalar_add(plan_f[0:1, 2 * EXPERTS + 1:], plan_f[0:1, 2 * EXPERTS:2 * EXPERTS + 1], -2.0))
            ch.mark(nc.vector.reduce_sum(plan_f[0:1, 0:EXPERTS], turn_n[:], axis=AX.X))
            ch.link(nc.vector.reduce_sum(plan_f[0:1, EXPERTS:2 * EXPERTS], turn_e[:], axis=AX.X))
            nc.vector.tensor_copy(plan[:], plan_f[:]).then_inc(plan_ready, 1)
            silu_times_up(last_pair)
            add_shared(last_pair)

            dve.wait_ge(plan_ready, 1)
            total = dve.value_load(plan[0:1, 2 * EXPERTS:2 * EXPERTS + 1], min_val=TOKENS * TOPK // P,
                                   max_val=TOKENS * TOPK // P + EXPERTS)
            start, per = ch.now(), 3 * KI
            with dve.Fori(0, total) as t:
                ch.body(start, t, per)
                silu_times_up(t + PAIRS)
                assert ch.n == per


def _constants():
    q = np.arange(P)
    c = np.zeros((P, C_ALL), np.float32)
    c[:, C_ID:C_ID + P] = np.eye(P)
    c[:, C_TRI:C_TRI + P] = q[:, None] < q[None, :]
    c[:, C_IOTA:C_IOTA + EXPERTS] = np.arange(EXPERTS)
    c[:, C_REGION:C_REGION + EXPERTS] = np.arange(EXPERTS) * REGION
    real = (q % HALF) < TEXT
    c[:, C_VALID] = real
    for k in range(TOPK):
        c[:, C_DUMP + k] = np.where(real, 0, DUMP + k * P + q)
    c[:, C_STEP] = np.where(real, 0, TOPK * P)
    c[:, C_TOK] = (q // HALF) * TEXT + np.minimum(q % HALF, TEXT - 1)
    c[:, C_THR:C_ALL] = np.arange(TILES_MAX) * P
    lists = np.zeros((P, DUMP // P, 2), np.int32)
    lists[:, :, 0] = TOKENS + np.arange(DUMP // P)[None, :] % P
    return c, lists.reshape(P, -1), np.zeros((HALF - TEXT, PAIRS, DIM), np.float32)


def kernel(**inputs):
    import concourse.bacc as _bacc
    from concourse.bass_utils import run_bass_kernel_spmd as _run

    a = {k: np.asarray(v) for k, v in inputs.items()}
    ctx = a["ctx_4096"]
    ctx_t = ctx.reshape(PAIRS, 2, ROW_TILE, ROW_TILES, KD, P).transpose(0, 4, 5, 1, 3, 2)

    def split(w):
        return w.reshape(KD, P, -1).transpose(1, 0, 2)

    def expert(wg, wu, wd):
        gu = np.stack([wg.swapaxes(-1, -2), wu.swapaxes(-1, -2)], -2)
        lead = gu.shape[:-3]
        gu = np.moveaxis(gu.reshape(*lead, KD, P, 2 * INNER), -3, -2).reshape(*lead, P, -1)
        dn = wd.swapaxes(-1, -2).reshape(*lead, KI, P, DIM)
        dn = np.moveaxis(dn, -3, -2).reshape(*lead, P, -1)
        return np.concatenate([gu, dn], -1)

    c, lists, pad = _constants()
    arrays = {
        "x": a["x"], "ctx": ctx, "ctx_t": ctx_t.reshape(PAIRS, KD, P, 2 * CTX),
        "wq_t": split(a["L0_xattn_Wq"].T), "bq": a["L0_xattn_bq"].reshape(KD, P).T,
        "wk": split(a["L0_xattn_Wk"]), "bk": a["L0_xattn_bk"].reshape(KD, P).T,
        "gate_t": split(a["L0_ffn_gate_w"].T), "gate_b": a["L0_ffn_bias"].reshape(1, EXPERTS),
        "experts": expert(a["L0_ffn_Wg"], a["L0_ffn_Wu"], a["L0_ffn_Wd"]),
        "shared": expert(a["L0_ffn_Sg"], a["L0_ffn_Su"], a["L0_ffn_Sd"]),
        "consts": c, "lists": lists, "pad": pad,
    }
    nc = _bacc.Bacc("TRN2", target_bir_lowering=False, num_devices=1)
    ins, aps = {}, {}
    for name, v in arrays.items():
        v = np.ascontiguousarray(v)
        ins[f"in_{name}"] = v
        aps[name] = nc.dram_tensor(f"in_{name}", v.shape, mybir.dt.from_np(v.dtype), kind="ExternalInput").ap()
    out = nc.dram_tensor("out_0", [TOKENS + P, DIM], mybir.dt.float32, kind="ExternalOutput").ap()
    moe_attention_kernel(nc, aps["x"], aps["ctx"], aps["ctx_t"], aps["wq_t"], aps["bq"], aps["wk"], aps["bk"],
                         aps["gate_t"], aps["gate_b"], aps["experts"], aps["shared"], aps["consts"],
                         (aps["lists"], aps["pad"]), out)
    r = _run(nc, [ins], core_ids=[0])
    return np.asarray(r.results[0]["out_0"])[:TOKENS].reshape(BATCH, TEXT, DIM)
```

```python
import concourse.bass as bass
from concourse import mybir
from contextlib import ExitStack
import numpy as np

BATCH, TEXT, DIM = 16, 56, 512
CTX = 1500
EXPERTS, INNER, TOPK = 16, 256, 4
P = 128
KD = DIM // P
KI = INNER // P
PAIRS = BATCH // 2
HALF = P // 2
PAIR_TOKENS = 2 * TEXT
TOKENS = BATCH * TEXT
ROW_TILE = 125
ROW_TILES = CTX // ROW_TILE
GROUPS = 3
PER_GROUP = ROW_TILES // GROUPS
CHUNKS = 3
CHUNK = CTX // CHUNKS
SPRAY = 112
SCALE = float(DIM) ** -0.5
EPS = 1e-5
REGION = 1024
TILES_MAX = -(-TOKENS // P)
DUMP = EXPERTS * REGION
SLOTS = 4
RING = 8
WFREE = KD * 2 * INNER + KI * DIM

C_ID, C_TRI, C_IOTA, C_REGION = 0, P, 2 * P, 2 * P + EXPERTS
C_VALID = C_REGION + EXPERTS
C_DUMP = C_VALID + 1
C_STEP = C_DUMP + TOPK
C_TOK = C_STEP + 1
C_THR = C_TOK + 1
C_ALL = C_THR + TILES_MAX


class Chain:

    def __init__(self, eng, sem):
        self.eng, self.sem, self.base, self.n = eng, sem, 0, 0

    def mark(self, ins):
        ins.then_inc(self.sem, 1)
        self.n += 1

    def link(self, ins):
        self.mark(ins)
        self.eng.wait_ge(self.sem, self.base + self.n)

    def body(self, start, i, per):
        self.base, self.n = start + i * per, 0

    def now(self):
        return self.base + self.n


def moe_attention_kernel(nc, x, ctx, ctx_t, wq, bq, wk, bk, gate_t, gate_b, experts, shared,
                         consts, entry_init, out):
    fp32, bf16 = mybir.dt.float32, mybir.dt.bfloat16
    i32, u32 = mybir.dt.int32, mybir.dt.uint32
    ALU, ACT, AX = mybir.AluOpType, mybir.ActivationFunctionType, mybir.AxisListType

    h_rows = nc.dram_tensor("h_rows", [TOKENS + P, DIM], fp32, kind="Internal").ap()
    entries = nc.dram_tensor("entries", [DUMP + PAIRS * TOPK * P, 2], i32, kind="Internal").ap()

    x_v = x.rearrange("(r b) t d -> b t r d", b=2)
    nat_v = ctx.rearrange("(r b) (p g c) d -> r g p b (c d)", b=2, g=GROUPS, c=PER_GROUP)

    es = ExitStack()
    with es:
        def sb(name, shape, dt=fp32):
            return es.enter_context(nc.sbuf_tensor(name, shape, dt))

        def sem(name):
            return es.enter_context(nc.semaphore(name))

        ctx_cols = sb("ctx_cols", [P, KD * 2 * CTX])
        ctx_rows = sb("ctx_rows", [P, GROUPS, 2, PER_GROUP * DIM])
        xs = sb("xs", [P, PAIRS, DIM])
        w_qk = sb("w_qk", [P, 2 * KD * DIM])
        w_fold = sb("w_fold", [P, KD, DIM])
        fold_cols = sb("fold_cols", [P, 2 * KD + 1])
        shared_sb = sb("shared_sb", [P, WFREE])
        gate_sb = sb("gate_sb", [P, KD, EXPERTS])
        gate_bias = sb("gate_bias", [P, EXPERTS])
        bq_sb = sb("bq_sb", [P, KD])
        bk_sb = sb("bk_sb", [P, KD])
        cst = sb("cst", [P, C_ALL])
        tri = sb("tri", [P, P], bf16)
        ones = sb("ones", [P, P], bf16)
        zero_rows = sb("zero_rows", [P, DIM])
        neg_half = sb("neg_half", [P, 1])
        xn = sb("xn", [P, DIM])
        xn_t = sb("xn_t", [P, KD, P])
        g_t = sb("g_t", [P, KD, P])
        probs = sb("probs", [P, CTX])
        probs_t = sb("probs_t", [P, ROW_TILES * P])
        h = sb("h", [P, DIM])
        h_t = sb("h_t", [P, KD, P])
        acc = sb("acc", [P, DIM])
        tanh_half = sb("tanh_half", [P, KI, P])
        gated = sb("gated", [P, KI, P])
        z = sb("z", [P, KI, P])
        stats = sb("stats", [P, 6])
        mean_var = sb("mean_var", [P, 2])
        var_eps = sb("var_eps", [P, 1])
        rstd = sb("rstd", [P, 1])
        row_max = sb("row_max", [P, 1])
        max_c = sb("max_c", [P, 1])
        exp_bias = sb("exp_bias", [P, 1])
        row_sum = sb("row_sum", [P, 1])
        row_inv = sb("row_inv", [P, 1])
        c_sb = sb("c_sb", [P, 1])
        g_exp = sb("g_exp", [P, EXPERTS])
        g_exp1 = sb("g_exp1", [P, EXPERTS])
        g_sig = sb("g_sig", [P, EXPERTS])
        g_score = sb("g_score", [P, EXPERTS])
        top = sb("top", [P, 8])
        top_i = sb("top_i", [P, 8], u32)
        top_f = sb("top_f", [P, TOPK])
        w_sum = sb("w_sum", [P, 1])
        w_inv = sb("w_inv", [P, 1])
        onehot = sb("onehot", [P, TOPK, EXPERTS])
        picked = sb("picked", [P, EXPERTS])
        mask = sb("mask", [P, EXPERTS], bf16)
        base = sb("base", [P, EXPERTS])
        rank = sb("rank", [P, EXPERTS])
        rank_sel = sb("rank_sel", [P, TOPK, EXPERTS])
        place_f = sb("place_f", [P, TOPK])
        place = sb("place", [P, TOPK], i32)
        dump_at = sb("dump_at", [P, TOPK])
        token = sb("token", [P, 1])
        entry = sb("entry", [P, TOPK, 2], i32)
        cnt = sb("cnt", [1, EXPERTS])
        above = sb("above", [1, EXPERTS, TILES_MAX])
        n_tiles = sb("n_tiles", [1, EXPERTS])
        active = sb("active", [1, EXPERTS])
        incl = sb("incl", [1, EXPERTS])
        excl = sb("excl", [1, EXPERTS])
        turn = sb("turn", [1, EXPERTS, EXPERTS])
        turn_on = sb("turn_on", [1, EXPERTS, EXPERTS])
        turn_n = sb("turn_n", [1, EXPERTS, EXPERTS])
        turn_e = sb("turn_e", [1, EXPERTS, EXPERTS])
        plan_f = sb("plan_f", [1, 2 * EXPERTS + 2])
        plan = sb("plan", [1, 2 * EXPERTS + 2], i32)
        ring = sb("ring", [P, RING, 2], i32)
        take_at = sb("take_at", [P, 1], i32)
        add_at = sb("add_at", [P, 1], i32)
        taken = sb("taken", [P, 2, DIM])
        taken_now = sb("taken_now", [P, DIM])
        taken_t = sb("taken_t", [P, KD, P])
        y_sb = sb("y_sb", [P, DIM])

        ident = cst[:, C_ID:C_ID + P]
        iota16 = cst[:, C_IOTA:C_IOTA + EXPERTS]
        region = cst[:, C_REGION:C_REGION + EXPERTS]
        valid = cst[:, C_VALID:C_VALID + 1]

        scores = es.enter_context(nc.psum_tensor("scores", [P, CHUNKS, 512], fp32))
        b3, b4, b5, b6, b7 = (es.enter_context(nc.psum_tensor(n, [P, 512], fp32))
                              for n in ("b3", "b4", "b5", "b6", "b7"))

        x_loaded, c_loaded = sem("x_loaded"), sem("c_loaded")
        wq_loaded, wk_loaded, sh_loaded = sem("wq_loaded"), sem("wk_loaded"), sem("sh_loaded")
        cols_loaded = [sem(f"cols_loaded{k}") for k in range(KD)]
        rows_loaded = [sem(f"rows_loaded{g}") for g in range(GROUPS)]
        cols_used, rows_used = sem("cols_used"), sem("rows_used")
        init_ready, init_stored = sem("init_ready"), sem("init_stored")
        var_ready, rstd_ready, xn_ready = sem("var_ready"), sem("rstd_ready"), sem("xn_ready")
        xt_ready, xnt_ready = sem("xt_ready"), sem("xnt_ready")
        fold_ready, folded, g_ready, gt_ready, c_read = (sem("fold_ready"), sem("folded"), sem("g_ready"),
                                                         sem("gt_ready"), sem("c_read"))
        scores_ready, bias_ready, probs_ready = sem("scores_ready"), sem("bias_ready"), sem("probs_ready")
        pt_ready, ptt_ready, attended_ready = sem("pt_ready"), sem("ptt_ready"), sem("attended_ready")
        x1_ready, h_ready, ht_ready, htt_ready = sem("x1_ready"), sem("h_ready"), sem("ht_ready"), sem("htt_ready")
        gate_ready, gexp_ready, mask_ready = sem("gate_ready"), sem("gexp_ready"), sem("mask_ready")
        rank_ready, rank_read, entries_ready = sem("rank_ready"), sem("rank_read"), sem("entries_ready")
        entries_stored, h_stored, acc_stored = sem("entries_stored"), sem("h_stored"), sem("acc_stored")
        up_ready, tanh_ready, z_ready, y_ready, acc_ready = (sem("up_ready"), sem("tanh_ready"), sem("z_ready"),
                                                             sem("y_ready"), sem("acc_ready"))
        plan_ready, entry_loaded, entry_free = sem("plan_ready"), sem("entry_loaded"), sem("entry_free")
        expert_loaded = [sem(f"expert_loaded{i}") for i in range(SLOTS)]
        gathered, now_ready, taken_used, tt_ready = (sem("gathered"), sem("now_ready"), sem("taken_used"),
                                                     sem("tt_ready"))
        ysb_ready, added = sem("ysb_ready"), sem("added")
        folded_half = sem("folded_half")
        waited = sem("waited")
        dve_step, pool_step = sem("dve_step"), sem("pool_step")

        block = es.enter_context(nc.Block())

        def settle(eng):
            eng.sem_inc(waited, 1)

        wq_sb = w_qk[:, 0:KD * DIM].rearrange("p (k n) -> p k n", k=KD)
        wk_sb = w_qk[:, KD * DIM:].rearrange("p (k n) -> p k n", k=KD)
        expert_w = [ctx_cols[:, i * WFREE:(i + 1) * WFREE] for i in range(SLOTS - 1)] + [w_qk[:, 0:WFREE]]

        @block.sync
        def _(sp):
            sp.sem_inc(entry_loaded, 16)
            sp.dma_start(cst[:], consts).then_inc(c_loaded, 16)
            sp.dma_start(wq_sb, wq).then_inc(wq_loaded, 16)
            sp.dma_start(wk_sb, wk).then_inc(wk_loaded, 16)
            sp.dma_start(bq_sb[:], bq).then_inc(wq_loaded, 16)
            sp.dma_start(bk_sb[:], bk).then_inc(wk_loaded, 16)
            for b in range(2):
                sp.dma_start(xs[HALF * b:HALF * b + TEXT, :, :], x_v[b]).then_inc(x_loaded, 16)
            for b in range(2):
                sp.dma_start(xs[HALF * b + TEXT:HALF * (b + 1), :, :], entry_init[1]).then_inc(x_loaded, 16)

            def load_cols(r, k):
                sp.dma_start(ctx_cols[:, k * 2 * CTX:(k + 1) * 2 * CTX],
                             ctx_t[bass.ds(r, 1), k, :, :].rearrange("a p n -> (a p) n")).then_inc(cols_loaded[k], 16)

            def load_rows(r, g):
                v = nat_v[bass.ds(r, 1), g, :, :, :].rearrange("a p b n -> (a p) b n")
                sp.dma_start(ctx_rows[0:SPRAY, g, :, :], v[0:SPRAY]).then_inc(rows_loaded[g], 16)
                sp.dma_start(ctx_rows[SPRAY:ROW_TILE, g, :, :], v[SPRAY:ROW_TILE]).then_inc(rows_loaded[g], 16)

            for k in range(KD):
                load_cols(0, k)
            for g in range(GROUPS):
                load_rows(0, g)
            sp.dma_start(gate_sb[:], gate_t).then_inc(sh_loaded, 16)
            sp.dma_start(gate_bias[:], gate_b.to_broadcast([P, EXPERTS])).then_inc(sh_loaded, 16)
            sp.dma_start(shared_sb[:], shared).then_inc(sh_loaded, 16)
            sp.wait_ge(init_ready, 1)
            sp.dma_start(h_rows[TOKENS:TOKENS + P, :], zero_rows[:]).then_inc(init_stored, 16)

            with sp.Fori(0, PAIRS - 1) as r:
                for k in range(KD):
                    sp.wait_ge(cols_used, r * KD + (k + 1))
                    load_cols(r + 1, k)
                for g in range(GROUPS):
                    sp.wait_ge(rows_used, r * GROUPS + (g + 1))
                    load_rows(r + 1, g)

            sp.wait_ge(cols_used, KD * PAIRS)
            sp.wait_ge(plan_ready, 1)
            t = sp.alloc_register("sp_tile")
            sp.reg_mov(t, 0)
            slot_tiles = [sp.alloc_register(f"sp_slot_tiles{i}") for i in range(SLOTS)]
            for reg in slot_tiles:
                sp.reg_mov(reg, 0)
            with sp.Fori(0, EXPERTS // SLOTS) as lap:
                for s in range(SLOTS):
                    n = sp.value_load(plan[0:1, bass.ds(lap * SLOTS + s, 1)], min_val=0, max_val=TILES_MAX)
                    e = sp.value_load(plan[0:1, bass.ds(lap * SLOTS + (EXPERTS + s), 1)], min_val=0, max_val=EXPERTS - 1)
                    with sp.If(n > 0):
                        sp.wait_ge(y_ready, sp.snap(slot_tiles[s], min_val=0, max_val=EXPERTS * TILES_MAX) + PAIRS)
                        sp.dma_start(expert_w[s], experts[bass.ds(e, 1), :, :].rearrange("a p n -> (a p) n")
                                     ).then_inc(expert_loaded[s], 16)
                        settle(sp)
                        sp.wait_ge(entries_stored, (PAIRS * TOPK + 1) * 16)
                        with sp.Fori(0, n) as j:
                            tv = sp.snap(t, min_val=0, max_val=EXPERTS * TILES_MAX)
                            free, loaded = sp.snap(tv + 1), sp.snap((tv + 1) * 16)
                            slot, at = sp.snap(tv % RING), sp.snap((e * (REGION // P) + j) * P)
                            sp.wait_ge(entry_free, free)
                            settle(sp)
                            sp.wait_ge(entry_loaded, loaded)
                            settle(sp)
                            sp.dma_start(ring[:, bass.ds(slot, 1), :].rearrange("p a c -> p (a c)"),
                                         entries[bass.ds(at, P), :]
                                         ).then_inc(entry_loaded, 16)
                            sp.reg_add(t, t, 1)
                        sp.reg_mov(slot_tiles[s], t)

        @block.gpsimd
        def _(pool):
            nc.gpsimd.memset(neg_half[:], -0.5).then_inc(pool_step, 1)
            nc.gpsimd.memset(zero_rows[:], 0.0).then_inc(init_ready, 1)
            pool.sem_inc(entry_free, RING)
            pool.wait_ge(pool_step, 1)

            pool.wait_ge(init_ready, 1)
            pool.dma_start(entries[0:DUMP, :].rearrange("(p n) c -> p (n c)", p=P), entry_init[0]
                           ).then_inc(entries_stored, 16)
            pool.dma_start(out[TOKENS:TOKENS + P, :], zero_rows[:]).then_inc(added, 16)

            def power(i):
                pool.wait_ge(var_ready, i + 1)
                nc.gpsimd.tensor_tensor(rstd[:], var_eps[:], neg_half[:], ALU.pow).then_inc(rstd_ready, 1)

            def scatter(r):
                pool.wait_ge(entries_ready, r + 1)
                settle(pool)
                for k in range(TOPK):
                    nc.gpsimd.indirect_dma_start(
                        entries[:, :], bass.IndirectOffsetOnAxis(ap=place[:, k:k + 1], axis=0),
                        entry[:, k, :], None).then_inc(entries_stored, 16)

            power(0)
            power(1)
            pool.wait_ge(entries_stored, 16)
            with pool.Fori(1, PAIRS - 1) as p:
                power(p * 2)
                power(p * 2 + 1)
                scatter(p - 1)
            power(2 * PAIRS - 2)
            scatter(PAIRS - 2)
            power(2 * PAIRS - 1)
            scatter(PAIRS - 1)

            pool.wait_ge(plan_ready, 1)
            lead = pool.value_load(plan[0:1, 2 * EXPERTS + 1:2 * EXPERTS + 2], min_val=TOKENS * TOPK // P - 2,
                                   max_val=TOKENS * TOPK // P + EXPERTS)
            pool.wait_ge(init_stored, 16)
            pool.wait_ge(h_stored, PAIRS * 32 + 16)
            pool.wait_ge(acc_stored, PAIRS * 32 + 16)

            def gather(t):
                pool.wait_ge(entry_loaded, (t + 2) * 16)
                nc.gpsimd.tensor_copy(take_at[:], ring[:, bass.ds(t % RING, 1), 0]).then_inc(pool_step, 1)

            def gather_start(t):
                if not isinstance(t, int):
                    pool.wait_ge(now_ready, t - 1)
                settle(pool)
                half = pool.snap(t % 2) if not isinstance(t, int) else None

                def start(i):
                    nc.gpsimd.indirect_dma_start(taken[:, i, :], None, h_rows[:, :],
                                                 bass.IndirectOffsetOnAxis(ap=take_at[:, 0:1], axis=0)
                                                 ).then_inc(gathered, 16)
                if half is None:
                    start(t % 2)
                else:
                    with pool.If(half > 0):
                        start(1)
                    with pool.If(half < 1):
                        start(0)

            def add(t):
                pool.wait_ge(added, (t + 1) * 16)
                settle(pool)
                nc.gpsimd.indirect_dma_start(out[:, :], bass.IndirectOffsetOnAxis(ap=add_at[:, 0:1], axis=0),
                                             y_sb[:], None, compute_op=ALU.add).then_inc(added, 16)

            def add_index(t):
                nc.gpsimd.tensor_copy(add_at[:], ring[:, bass.ds(t % RING, 1), 0]).then_inc(entry_free, 1)

            def take(t):
                pool.wait_ge(gathered, t * 16)
                gather(t)
                pool.wait_ge(pool_step, t + 2)
                gather_start(t)

            def give(t):
                pool.wait_ge(added, (t + 1) * 16)
                pool.wait_ge(ysb_ready, t + 2)
                add_index(t)
                pool.wait_ge(entry_free, t + (RING + 1))
                add(t)

            take(0)
            take(1)
            with pool.Fori(0, lead) as t:
                take(t + 2)
                give(t)
            pool.wait_ge(gathered, (lead + 2) * 16)
            gather_start(lead + 2)
            give(lead)
            give(lead + 1)
            pool.wait_ge(added, (lead + 3) * 16)
            pool.wait_ge(gathered, (lead + 3) * 16)

        @block.tensor
        def _(pe):
            def transposes(bank, src):
                for k in range(KD):
                    last = nc.tensor.transpose(bank[:, k * P:(k + 1) * P], src[:, k * P:(k + 1) * P], ident)
                return last

            def x_transpose(p, bank):
                pe.wait_ge(xn_ready, p + 1)
                transposes(bank, xn).then_inc(xt_ready, 1)

            def fold():
                pe.wait_ge(wq_loaded, 32)
                pe.wait_ge(wk_loaded, 32)
                for m, bank in enumerate((scores[:, 0, :], scores[:, 1, :], scores[:, 2, :], b6[:, :])):
                    for k in range(KD):
                        last = nc.tensor.matmul(bank, wq_sb[:, k, m * P:(m + 1) * P], wk_sb[:, k, :],
                                                start=(k == 0), stop=(k == KD - 1))
                    last.then_inc(fold_ready, 1)
                for col in range(2 * KD):
                    w, vec = ((wk_sb, bq_sb), (wq_sb, bk_sb))[col // KD]
                    at = col % KD * P
                    for k in range(KD):
                        nc.tensor.matmul(b7[:, col:col + 1], w[:, k, at:at + P], vec[:, k:k + 1],
                                         start=(k == 0), stop=(k == KD - 1))
                for k in range(KD):
                    last = nc.tensor.matmul(b7[:, 2 * KD:2 * KD + 1], bq_sb[:, k:k + 1].to_broadcast([P, P]),
                                            bk_sb[:, k:k + 1], start=(k == 0), stop=(k == KD - 1))
                last.then_inc(fold_ready, 1)

            def project(p):
                pe.wait_ge(xnt_ready, p + 1)
                for m in range(KD):
                    for k in range(KD):
                        last = nc.tensor.matmul(b7[:, m * P:(m + 1) * P], w_fold[:, k, m * P:(m + 1) * P],
                                                xn_t[:, k, :], start=(k == 0), stop=(k == KD - 1))
                last.then_inc(g_ready, 1)

            def project_bias(p):
                for k in range(KD):
                    last = nc.tensor.matmul(b3[:, 32:33], xn_t[:, k, :], fold_cols[:, KD + k:KD + k + 1],
                                            start=(k == 0), stop=(k == KD - 1))
                last.then_inc(g_ready, 1)

            def score(p):
                pe.wait_ge(gt_ready, p + 1)
                pe.wait_ge(probs_ready, p)
                for k in range(KD):
                    pe.wait_ge(cols_loaded[k], (p + 1) * 16)
                    for n in range(CHUNKS):
                        for b in range(2):
                            at = (2 * k + b) * CTX + n * CHUNK
                            last = nc.tensor.matmul(scores[HALF * b:HALF * (b + 1), n, 0:CHUNK],
                                                    g_t[:, k, HALF * b:HALF * (b + 1)],
                                                    ctx_cols[:, at:at + CHUNK],
                                                    start=(k == 0), stop=(k == KD - 1))
                    last.then_inc(cols_used, 1)

            def transpose_probs(p, g):
                bank = (b4, b5)[g % 2]
                if g == 0:
                    pe.wait_ge(probs_ready, p + 1)
                if g == 2:
                    pe.wait_ge(ptt_ready, p * GROUPS + 1)
                for c in range(PER_GROUP):
                    at = (g * PER_GROUP + c) * ROW_TILE
                    last = nc.tensor.transpose(bank[0:ROW_TILE, c * P:(c + 1) * P],
                                               probs[:, at:at + ROW_TILE], ident)
                last.then_inc(pt_ready, 1)

            def attend(p):
                for g in range(GROUPS):
                    pe.wait_ge(ptt_ready, p * GROUPS + (g + 1))
                    pe.wait_ge(rows_loaded[g], (p + 1) * 32)
                    for c in range(PER_GROUP):
                        for b in range(2):
                            at = (g * PER_GROUP + c) * P + HALF * b
                            first, end = g + c == 0, g * PER_GROUP + c == ROW_TILES - 1
                            last = nc.tensor.matmul(b3[HALF * b:HALF * (b + 1), :],
                                                    probs_t[0:ROW_TILE, at:at + HALF],
                                                    ctx_rows[0:ROW_TILE, g, b, c * DIM:(c + 1) * DIM],
                                                    start=first, stop=end)
                    last.then_inc(rows_used, 1)

            def h_transpose(r):
                pe.wait_ge(h_ready, r + 1)
                transposes(b4, h).then_inc(ht_ready, 1)

            def gate(r):
                pe.wait_ge(htt_ready, r + 1)
                for k in range(KD):
                    last = nc.tensor.matmul(b3[:, 0:EXPERTS], h_t[:, k, :], gate_sb[:, k, :],
                                            start=(k == 0), stop=(k == KD - 1))
                last.then_inc(gate_ready, 1)

            def ranks(r):
                pe.wait_ge(mask_ready, r + 1)
                nc.tensor.matmul(scores[:, 0, 0:EXPERTS], tri[:], mask[:], start=True, stop=True)
                nc.tensor.matmul(scores[:, 0, EXPERTS:2 * EXPERTS], ones[:], mask[:], start=True, stop=True
                                 ).then_inc(rank_ready, 1)

            def up(w, src_t):
                for i in range(KI):
                    bank = (b6, b7)[i]
                    for half in range(2):
                        for k in range(KD):
                            at = (2 * k + half) * INNER + i * P
                            last = nc.tensor.matmul(bank[:, half * P:(half + 1) * P], w[:, at:at + P],
                                                    src_t[:, k, :], start=(k == 0), stop=(k == KD - 1))
                    last.then_inc(up_ready, 1)

            def down(w, uses):
                for i in range(KI):
                    pe.wait_ge(z_ready, uses * KI + (i + 1))
                    at = KD * 2 * INNER + i * DIM
                    last = nc.tensor.matmul(b3[:, :], z[:, i, :], w[:, at:at + DIM],
                                            start=(i == 0), stop=(i == KI - 1))
                last.then_inc(y_ready, 1)

            pe.sem_inc(ht_ready, 1)
            fold()
            pe.wait_ge(c_loaded, 16)
            x_transpose(0, b5)
            pe.wait_ge(folded, 1)
            project(0)
            project_bias(0)
            score(0)
            x_transpose(1, b5)
            pe.wait_ge(gt_ready, 1)
            project(1)
            pe.wait_ge(c_read, 1)
            project_bias(1)
            for g in range(GROUPS):
                transpose_probs(0, g)
            pe.wait_ge(sh_loaded, 48)
            pe.wait_ge(c_read, 2)
            attend(0)
            with pe.Fori(1, PAIRS - 1) as p:
                score(p)
                h_transpose(p - 1)
                x_transpose(p + 1, b5)
                gate(p - 1)
                project(p + 1)
                pe.wait_ge(gexp_ready, p)
                project_bias(p + 1)
                pe.wait_ge(gt_ready, p + 2)
                up(shared_sb, h_t)
                pe.wait_ge(probs_ready, p + 1)
                ranks(p - 1)
                transpose_probs(p, 0)
                transpose_probs(p, 1)
                pe.wait_ge(c_read, p + 2)
                down(shared_sb, p - 1)
                transpose_probs(p, 2)
                pe.wait_ge(acc_ready, p)
                attend(p)
                pe.wait_ge(rank_read, p)
            last_pair = PAIRS - 1
            score(last_pair)
            h_transpose(last_pair - 1)
            gate(last_pair - 1)
            up(shared_sb, h_t)
            pe.wait_ge(probs_ready, PAIRS)
            ranks(last_pair - 1)
            transpose_probs(last_pair, 0)
            transpose_probs(last_pair, 1)
            transpose_probs(last_pair, 2)
            pe.wait_ge(gexp_ready, last_pair)
            attend(last_pair)
            pe.wait_ge(x1_ready, PAIRS)
            down(shared_sb, last_pair - 1)
            h_transpose(last_pair)
            pe.wait_ge(acc_ready, last_pair)
            gate(last_pair)
            pe.wait_ge(rank_read, last_pair)
            ranks(last_pair)
            up(shared_sb, h_t)
            pe.wait_ge(gexp_ready, PAIRS)
            down(shared_sb, last_pair)

            def tile_transpose(t):
                pe.wait_ge(now_ready, t + 1)
                transposes(b4, taken_now).then_inc(taken_used, 1)

            pe.wait_ge(plan_ready, 1)
            t = pe.alloc_register("pe_tile")
            pe.reg_mov(t, 0)
            tile_transpose(0)
            with pe.Fori(0, EXPERTS // SLOTS) as lap:
                for s in range(SLOTS):
                    n = pe.value_load(plan[0:1, bass.ds(lap * SLOTS + s, 1)], min_val=0, max_val=TILES_MAX)
                    with pe.If(n > 0):
                        pe.wait_ge(expert_loaded[s], (lap + 1) * 16)
                        settle(pe)
                        with pe.Fori(0, n) as j:
                            tv = pe.snap(t, min_val=0, max_val=EXPERTS * TILES_MAX)
                            pe.wait_ge(tt_ready, tv + 1)
                            up(expert_w[s], taken_t)
                            tile_transpose(tv + 1)
                            pe.wait_ge(acc_ready, PAIRS)
                            pe.wait_ge(ysb_ready, tv + 1)
                            down(expert_w[s], tv + PAIRS)
                            pe.reg_add(t, t, 1)

        @block.scalar
        def _(act):
            def copy_x_t(p, bank):
                act.wait_ge(xt_ready, p + 1)
                nc.scalar.copy(xn_t[:].rearrange("p k n -> p (k n)"), bank[:, :]).then_inc(xnt_ready, 1)

            def softmax(p):
                act.wait_ge(bias_ready, p + 1)
                nc.scalar.activation(probs[:].rearrange("p (n c) -> p n c", n=CHUNKS), scores[:, :, 0:CHUNK],
                                     ACT.Exp, bias=exp_bias[:], scale=SCALE, accum_out=row_sum[:]
                                     ).then_inc(probs_ready, 1)

            def copy_probs_t(p):
                for g in range(GROUPS):
                    act.wait_ge(pt_ready, p * GROUPS + (g + 1))
                    nc.scalar.copy(probs_t[0:ROW_TILE, g * PER_GROUP * P:(g + 1) * PER_GROUP * P],
                                   (b4, b5)[g % 2][0:ROW_TILE, :]).then_inc(ptt_ready, 1)

            def copy_h_t(r):
                act.wait_ge(ht_ready, r + 2)
                nc.scalar.copy(h_t[:].rearrange("p k n -> p (k n)"), b4[:, :]).then_inc(htt_ready, 1)

            def store_pair(r, src, dst, done):
                for b in range(2):
                    act.dma_start(dst[bass.ds(r * PAIR_TOKENS + b * TEXT, TEXT), :],
                                  src[HALF * b:HALF * b + TEXT, :]).then_inc(done, 16)

            def gate_exp(r):
                act.wait_ge(gate_ready, r + 1)
                nc.scalar.activation(g_exp[:], b3[:, 0:EXPERTS], ACT.Exp, scale=-1.0).then_inc(gexp_ready, 1)

            def up_tanh(uses):
                for i in range(KI):
                    act.wait_ge(up_ready, uses * KI + (i + 1))
                    nc.scalar.activation(tanh_half[:, i, :], (b6, b7)[i][:, 0:P], ACT.Tanh, scale=0.5
                                         ).then_inc(tanh_ready, 1)

            for done, n in ((h_stored, 16), (acc_stored, 16), (ysb_ready, 1)):
                act.sem_inc(done, n)
            for m in range(2):
                act.wait_ge(fold_ready, m + 1)
                nc.scalar.copy(w_fold[:, m, :], scores[:, m, :]).then_inc(folded_half, 1)
            copy_x_t(0, b5)
            copy_x_t(1, b5)
            softmax(0)
            copy_probs_t(0)
            with act.Fori(1, PAIRS - 1) as p:
                act.wait_ge(h_ready, p)
                store_pair(p - 1, h, h_rows, h_stored)
                copy_h_t(p - 1)
                copy_x_t(p + 1, b5)
                gate_exp(p - 1)
                softmax(p)
                up_tanh(p - 1)
                copy_probs_t(p)
                act.wait_ge(acc_ready, p)
                store_pair(p - 1, acc, out, acc_stored)
            last_pair = PAIRS - 1
            act.wait_ge(h_ready, last_pair)
            store_pair(last_pair - 1, h, h_rows, h_stored)
            copy_h_t(last_pair - 1)
            gate_exp(last_pair - 1)
            softmax(last_pair)
            up_tanh(last_pair - 1)
            copy_probs_t(last_pair)
            act.wait_ge(h_ready, PAIRS)
            store_pair(last_pair, h, h_rows, h_stored)
            copy_h_t(last_pair)
            act.wait_ge(acc_ready, last_pair)
            store_pair(last_pair - 1, acc, out, acc_stored)
            gate_exp(last_pair)
            up_tanh(last_pair)
            act.wait_ge(acc_ready, PAIRS)
            store_pair(last_pair, acc, out, acc_stored)

            act.wait_ge(plan_ready, 1)
            total = act.value_load(plan[0:1, 2 * EXPERTS:2 * EXPERTS + 1], min_val=TOKENS * TOPK // P,
                                   max_val=TOKENS * TOPK // P + EXPERTS)

            def copy_taken_t(t):
                act.wait_ge(taken_used, t + 1)
                nc.scalar.copy(taken_t[:].rearrange("p k n -> p (k n)"), b4[:, :]).then_inc(tt_ready, 1)

            copy_taken_t(0)
            with act.Fori(0, total) as t:
                up_tanh(t + PAIRS)
                copy_taken_t(t + 1)
                act.wait_ge(y_ready, t + (PAIRS + 1))
                act.wait_ge(added, (t + 1) * 16)
                act.wait_ge(entry_loaded, (t + 2) * 16)
                nc.scalar.activation(y_sb[:], b3[:, :], ACT.Copy,
                                     scale=ring[:, bass.ds(t % RING, 1), 1].bitcast(fp32)).then_inc(ysb_ready, 1)

        @block.vector
        def _(dve):
            ch = Chain(dve, dve_step)

            def normalise(i, src, dst, done):
                settle(dve)
                ch.link(nc.vector.bn_stats(stats[:], src))
                settle(dve)
                ch.link(nc.vector.bn_aggr(mean_var[:], stats[:]))
                nc.vector.tensor_scalar_add(var_eps[:], mean_var[:, 1:2], EPS).then_inc(var_ready, 1)
                dve.wait_ge(rstd_ready, i + 1)
                nc.vector.tensor_scalar(dst[:], src, mean_var[:, 0:1], rstd[:], ALU.subtract, ALU.mult
                                        ).then_inc(done, 1)

            def pair_x(p):
                return xs[:, bass.ds(p, 1), :].rearrange("p a n -> p (a n)")

            def norm_x(p, i):
                if not isinstance(p, int) or p > 0:
                    dve.wait_ge(xt_ready, p)
                normalise(i, pair_x(p), xn, xn_ready)

            def finish_attention(r, i):
                dve.wait_ge(probs_ready, r + 1)
                ch.link(nc.vector.reciprocal(row_inv[:], row_sum[:]))
                dve.wait_ge(rows_used, (r + 1) * GROUPS)
                nc.vector.scalar_tensor_tensor(pair_x(r), b3[:, :], row_inv[:], pair_x(r), ALU.mult, ALU.add
                                               ).then_inc(x1_ready, 1)
                dve.wait_ge(x1_ready, r + 1)
                dve.wait_ge(h_stored, r * 32 + 16)
                dve.wait_ge(ht_ready, r + 1)
                normalise(i, pair_x(r), h, h_ready)

            def score_max(p):
                dve.wait_ge(cols_used, (p + 1) * KD)
                ch.link(nc.vector.reduce_max(row_max[:], scores[:, :, 0:CHUNK], axis=AX.XY))
                dve.wait_ge(c_read, p + 1)
                ch.link(nc.vector.tensor_scalar(max_c[:], row_max[:], c_sb[:], -SCALE, ALU.add, ALU.mult))
                nc.vector.scalar_tensor_tensor(exp_bias[:], c_sb[:], SCALE, max_c[:], ALU.mult, ALU.add
                                               ).then_inc(bias_ready, 1)

            def add_g_bias(p):
                dve.wait_ge(g_ready, 2 * p + 1)
                nc.vector.tensor_tensor(g_t[:], b7[:, :].rearrange("p (k n) -> p k n", k=KD),
                                        fold_cols[:, 0:KD].unsqueeze(2).to_broadcast([P, KD, P]), ALU.add
                                        ).then_inc(gt_ready, 1)

            def read_c(p):
                dve.wait_ge(g_ready, 2 * p + 2)
                dve.wait_ge(bias_ready, p)
                nc.vector.tensor_tensor(c_sb[:], b3[:, 32:33], fold_cols[:, 2 * KD:], ALU.add).then_inc(c_read, 1)

            def route(r):
                dve.wait_ge(gexp_ready, r + 1)
                ch.link(nc.vector.tensor_scalar_add(g_exp1[:], g_exp[:], 1.0))
                ch.link(nc.vector.reciprocal(g_sig[:], g_exp1[:]))
                ch.link(nc.vector.tensor_tensor(g_score[:], g_sig[:], gate_bias[:], ALU.add))
                settle(dve)
                ch.link(nc.vector.max(top[:], g_score[:]))
                settle(dve)
                ch.link(nc.vector.max_index(top_i[:], top[:], g_score[:]))
                ch.mark(nc.vector.reduce_sum(w_sum[:], top[:, 0:TOPK], axis=AX.X))
                ch.link(nc.vector.tensor_copy(top_f[:], top_i[:, 0:TOPK]))
                ch.link(nc.vector.tensor_tensor(onehot[:], iota16.unsqueeze(1).to_broadcast([P, TOPK, EXPERTS]),
                                                top_f[:].unsqueeze(2).to_broadcast([P, TOPK, EXPERTS]),
                                                ALU.is_equal))
                ch.link(nc.vector.reduce_sum(picked[:], onehot[:].rearrange("p k e -> p e k"), axis=AX.X))
                nc.vector.tensor_scalar(mask[:], picked[:], valid, None, ALU.mult).then_inc(mask_ready, 1)
                ch.link(nc.vector.tensor_scalar_add(w_inv[:], w_sum[:], 1e-20))
                ch.link(nc.vector.reciprocal(w_sum[:], w_inv[:]))
                dve.wait_ge(entries_stored, r * (TOPK * 16) + 16)
                nc.vector.tensor_scalar(entry[:, :, 1].bitcast(fp32), top[:, 0:TOPK], w_sum[:], None, ALU.mult)

            def enter(r):
                dve.wait_ge(rank_ready, r + 1)
                nc.vector.tensor_tensor(rank[:], scores[:, 0, 0:EXPERTS], base[:], ALU.add)
                ch.mark(nc.vector.tensor_tensor(base[:], scores[:, 0, EXPERTS:2 * EXPERTS], base[:], ALU.add))
                ch.link(nc.vector.tensor_copy(entry[:, :, 0], token[:].to_broadcast([P, TOPK])))
                ch.link(nc.vector.tensor_tensor(rank_sel[:], onehot[:],
                                                rank[:].unsqueeze(1).to_broadcast([P, TOPK, EXPERTS]), ALU.mult))
                ch.link(nc.vector.reduce_sum(place_f[:], rank_sel[:], axis=AX.X))
                nc.vector.scalar_tensor_tensor(place[:], place_f[:], valid, dump_at[:], ALU.mult, ALU.add
                                               ).then_inc(entries_ready, 1)
                nc.vector.tensor_scalar(dump_at[:], dump_at[:], cst[:, C_STEP:C_STEP + 1], None, ALU.add)
                nc.vector.tensor_scalar_add(token[:], token[:], float(PAIR_TOKENS)).then_inc(rank_read, 1)

            def silu_times_up(uses):
                for i in range(KI):
                    bank = (b6, b7)[i]
                    dve.wait_ge(tanh_ready, uses * KI + (i + 1))
                    ch.link(nc.vector.scalar_tensor_tensor(gated[:, i, :], tanh_half[:, i, :], 1.0, bank[:, 0:P],
                                                           ALU.add, ALU.mult))
                    nc.vector.scalar_tensor_tensor(z[:, i, :], gated[:, i, :], 0.5, bank[:, P:2 * P],
                                                   ALU.mult, ALU.mult).then_inc(z_ready, 1)

            def add_shared(r):
                dve.wait_ge(y_ready, r + 1)
                dve.wait_ge(acc_stored, r * 32 + 16)
                nc.vector.tensor_tensor(acc[:], b3[:, :], pair_x(r), ALU.add).then_inc(acc_ready, 1)

            dve.wait_ge(c_loaded, 16)
            nc.vector.tensor_copy(tri[:], cst[:, C_TRI:C_TRI + P])
            nc.vector.memset(ones[:], 1.0)
            nc.vector.tensor_copy(base[:], region)
            nc.vector.tensor_copy(dump_at[:], cst[:, C_DUMP:C_DUMP + TOPK])
            ch.link(nc.vector.tensor_copy(token[:], cst[:, C_TOK:C_TOK + 1]))
            dve.wait_ge(x_loaded, 64)
            norm_x(0, 0)
            for m, bank in ((2, scores[:, 2, :]), (3, b6[:, :])):
                dve.wait_ge(fold_ready, m + 1)
                nc.vector.tensor_copy(w_fold[:, m, :], bank)
            dve.wait_ge(fold_ready, KD + 1)
            dve.wait_ge(folded_half, 2)
            nc.vector.tensor_copy(fold_cols[:], b7[:, 0:2 * KD + 1]).then_inc(folded, 1)
            dve.wait_ge(folded, 1)
            add_g_bias(0)
            read_c(0)
            norm_x(1, 1)
            score_max(0)
            add_g_bias(1)
            read_c(1)
            dve.wait_ge(sh_loaded, 48)

            def body(p):
                finish_attention(p - 1, p * 2)
                if not isinstance(p, int):
                    norm_x(p + 1, p * 2 + 1)
                score_max(p)
                route(p - 1)
                if not isinstance(p, int):
                    add_g_bias(p + 1)
                    read_c(p + 1)

            start, per = ch.now(), 24
            with dve.Fori(1, PAIRS - 1) as p:
                ch.body(start, p - 1, per)
                body(p)
                silu_times_up(p - 1)
                add_shared(p - 1)
                enter(p - 1)
                assert ch.n == per, ch.n
            last_pair = PAIRS - 1
            ch.base, ch.n = start + (PAIRS - 2) * per, 0
            body(last_pair)
            silu_times_up(last_pair - 1)
            enter(last_pair - 1)
            finish_attention(last_pair, 2 * PAIRS - 1)
            add_shared(last_pair - 1)
            route(last_pair)
            enter(last_pair)

            dve.wait_ge(rank_read, PAIRS)
            ch.link(nc.vector.tensor_tensor(cnt[:], base[0:1, :], region[0:1, :], ALU.subtract))
            ch.link(nc.vector.tensor_tensor(above[:], cnt[:].unsqueeze(2).to_broadcast([1, EXPERTS, TILES_MAX]),
                                            cst[0:1, C_THR:C_ALL].unsqueeze(1).to_broadcast([1, EXPERTS, TILES_MAX]),
                                            ALU.is_gt))
            ch.link(nc.vector.reduce_sum(n_tiles[:], above[:], axis=AX.X))
            ch.mark(nc.vector.reduce_sum(plan_f[0:1, 2 * EXPERTS:2 * EXPERTS + 1], n_tiles[:], axis=AX.X))
            ch.link(nc.vector.tensor_scalar_min(active[:], n_tiles[:], 1.0))
            ch.link(nc.vector.tensor_tensor_scan(incl[:], cst[0:1, C_ID:C_ID + 1].to_broadcast([1, EXPERTS]),
                                                 active[:], 0.0, ALU.mult, ALU.add))
            ch.link(nc.vector.tensor_tensor(excl[:], incl[:], active[:], ALU.subtract))
            wide = [1, EXPERTS, EXPERTS]
            ch.link(nc.vector.tensor_tensor(turn[:], excl[:].unsqueeze(1).to_broadcast(wide),
                                            iota16[0:1, :].unsqueeze(2).to_broadcast(wide), ALU.is_equal))
            ch.link(nc.vector.tensor_tensor(turn_on[:], turn[:], active[:].unsqueeze(1).to_broadcast(wide), ALU.mult))
            ch.mark(nc.vector.tensor_tensor(turn_n[:], turn_on[:], n_tiles[:].unsqueeze(1).to_broadcast(wide), ALU.mult))
            ch.link(nc.vector.tensor_tensor(turn_e[:], turn_on[:], iota16[0:1, :].unsqueeze(1).to_broadcast(wide),
                                            ALU.mult))
            ch.mark(nc.vector.tensor_scalar_add(plan_f[0:1, 2 * EXPERTS + 1:], plan_f[0:1, 2 * EXPERTS:2 * EXPERTS + 1], -2.0))
            ch.mark(nc.vector.reduce_sum(plan_f[0:1, 0:EXPERTS], turn_n[:], axis=AX.X))
            ch.link(nc.vector.reduce_sum(plan_f[0:1, EXPERTS:2 * EXPERTS], turn_e[:], axis=AX.X))
            nc.vector.tensor_copy(plan[:], plan_f[:]).then_inc(plan_ready, 1)
            silu_times_up(last_pair)
            add_shared(last_pair)

            dve.wait_ge(plan_ready, 1)
            total = dve.value_load(plan[0:1, 2 * EXPERTS:2 * EXPERTS + 1], min_val=TOKENS * TOPK // P,
                                   max_val=TOKENS * TOPK // P + EXPERTS)
            def copy_taken(t):
                dve.wait_ge(gathered, (t + 1) * 16)
                if not isinstance(t, int):
                    dve.wait_ge(taken_used, t)
                nc.vector.tensor_copy(taken_now[:], taken[:, bass.ds(t % 2, 1), :].rearrange("p a n -> p (a n)")
                                      ).then_inc(now_ready, 1)

            copy_taken(0)
            start, per = ch.now(), KI
            with dve.Fori(0, total) as t:
                ch.body(start, t, per)
                copy_taken(t + 1)
                silu_times_up(t + PAIRS)
                assert ch.n == per


def _constants():
    q = np.arange(P)
    c = np.zeros((P, C_ALL), np.float32)
    c[:, C_ID:C_ID + P] = np.eye(P)
    c[:, C_TRI:C_TRI + P] = q[:, None] < q[None, :]
    c[:, C_IOTA:C_IOTA + EXPERTS] = np.arange(EXPERTS)
    c[:, C_REGION:C_REGION + EXPERTS] = np.arange(EXPERTS) * REGION
    real = (q % HALF) < TEXT
    c[:, C_VALID] = real
    for k in range(TOPK):
        c[:, C_DUMP + k] = np.where(real, 0, DUMP + k * P + q)
    c[:, C_STEP] = np.where(real, 0, TOPK * P)
    c[:, C_TOK] = (q // HALF) * TEXT + np.minimum(q % HALF, TEXT - 1)
    c[:, C_THR:C_ALL] = np.arange(TILES_MAX) * P
    lists = np.zeros((P, DUMP // P, 2), np.int32)
    lists[:, :, 0] = TOKENS + np.arange(DUMP // P)[None, :] % P
    return c, lists.reshape(P, -1), np.zeros((HALF - TEXT, PAIRS, DIM), np.float32)


def kernel(**inputs):
    import concourse.bacc as _bacc
    from concourse.bass_utils import run_bass_kernel_spmd as _run

    a = {k: np.asarray(v) for k, v in inputs.items()}
    ctx = a["ctx_4096"]
    ctx_t = ctx.reshape(PAIRS, 2, ROW_TILE, ROW_TILES, KD, P).transpose(0, 4, 5, 1, 3, 2)

    def split(w):
        return w.reshape(KD, P, -1).transpose(1, 0, 2)

    def expert(wg, wu, wd):
        gu = np.stack([wg.swapaxes(-1, -2), wu.swapaxes(-1, -2)], -2)
        lead = gu.shape[:-3]
        gu = np.moveaxis(gu.reshape(*lead, KD, P, 2 * INNER), -3, -2).reshape(*lead, P, -1)
        dn = wd.swapaxes(-1, -2).reshape(*lead, KI, P, DIM)
        dn = np.moveaxis(dn, -3, -2).reshape(*lead, P, -1)
        return np.concatenate([gu, dn], -1)

    c, lists, pad = _constants()
    arrays = {
        "x": a["x"], "ctx": ctx, "ctx_t": ctx_t.reshape(PAIRS, KD, P, 2 * CTX),
        "wq": split(a["L0_xattn_Wq"]), "bq": a["L0_xattn_bq"].reshape(KD, P).T,
        "wk": split(a["L0_xattn_Wk"]), "bk": a["L0_xattn_bk"].reshape(KD, P).T,
        "gate_t": split(a["L0_ffn_gate_w"].T), "gate_b": a["L0_ffn_bias"].reshape(1, EXPERTS),
        "experts": expert(a["L0_ffn_Wg"], a["L0_ffn_Wu"], a["L0_ffn_Wd"]),
        "shared": expert(a["L0_ffn_Sg"], a["L0_ffn_Su"], a["L0_ffn_Sd"]),
        "consts": c, "lists": lists, "pad": pad,
    }
    nc = _bacc.Bacc("TRN2", target_bir_lowering=False, num_devices=1)
    ins, aps = {}, {}
    for name, v in arrays.items():
        v = np.ascontiguousarray(v)
        ins[f"in_{name}"] = v
        aps[name] = nc.dram_tensor(f"in_{name}", v.shape, mybir.dt.from_np(v.dtype), kind="ExternalInput").ap()
    out = nc.dram_tensor("out_0", [TOKENS + P, DIM], mybir.dt.float32, kind="ExternalOutput").ap()
    moe_attention_kernel(nc, aps["x"], aps["ctx"], aps["ctx_t"], aps["wq"], aps["bq"], aps["wk"], aps["bk"],
                         aps["gate_t"], aps["gate_b"], aps["experts"], aps["shared"], aps["consts"],
                         (aps["lists"], aps["pad"]), out)
    r = _run(nc, [ins], core_ids=[0])
    return np.asarray(r.results[0]["out_0"])[:TOKENS].reshape(BATCH, TEXT, DIM)
```

```python
import concourse.bass as bass
from concourse import mybir
from contextlib import ExitStack
import numpy as np

BATCH, TEXT, DIM = 16, 56, 512
CTX = 1500
EXPERTS, INNER, TOPK = 16, 256, 4
P = 128
KD = DIM // P
KI = INNER // P
PAIRS = BATCH // 2
HALF = P // 2
PAIR_TOKENS = 2 * TEXT
TOKENS = BATCH * TEXT
ROW_TILE = 125
ROW_TILES = CTX // ROW_TILE
GROUPS = 3
PER_GROUP = ROW_TILES // GROUPS
CHUNKS = 3
CHUNK = CTX // CHUNKS
SPRAY = 112
SCALE = float(DIM) ** -0.5
EPS = 1e-5
REGION = 1024
TILES_MAX = -(-TOKENS // P)
DUMP = EXPERTS * REGION
SLOTS = 4
HELD = 4
AHEAD = 5
RING = 16
WFREE = KD * 2 * INNER + KI * DIM
UP, DOWN = KD * 2 * INNER, KI * DIM
PIECES = KD + KI
FIRST, SECOND, THIRD = (range(i * PIECES // 3, (i + 1) * PIECES // 3) for i in range(3))

C_ID, C_TRI, C_IOTA, C_REGION = 0, P, 2 * P, 2 * P + EXPERTS
C_VALID = C_REGION + EXPERTS
C_DUMP = C_VALID + 1
C_STEP = C_DUMP + TOPK
C_TOK = C_STEP + 1
C_THR = C_TOK + 1
C_ALL = C_THR + TILES_MAX


class Chain:

    def __init__(self, eng, sem):
        self.eng, self.sem, self.base, self.n = eng, sem, 0, 0

    def mark(self, ins):
        ins.then_inc(self.sem, 1)
        self.n += 1

    def link(self, ins):
        self.mark(ins)
        self.eng.wait_ge(self.sem, self.base + self.n)

    def body(self, start, i, per):
        self.base, self.n = start + i * per, 0

    def now(self):
        return self.base + self.n


def moe_attention_kernel(nc, x, ctx, ctx_t, wq, bq, wk, bk, gate_t, gate_b, experts, shared,
                         consts, entry_init, out):
    fp32, bf16 = mybir.dt.float32, mybir.dt.bfloat16
    f32r = mybir.dt.float32r
    i32, u32 = mybir.dt.int32, mybir.dt.uint32
    ALU, ACT, AX = mybir.AluOpType, mybir.ActivationFunctionType, mybir.AxisListType

    h_rows = nc.dram_tensor("h_rows", [TOKENS + P, DIM], fp32, kind="Internal").ap()
    entries = nc.dram_tensor("entries", [DUMP + PAIRS * TOPK * P, 2], i32, kind="Internal").ap()

    x_v = x.rearrange("(r b) t d -> b t r d", b=2)
    nat_v = ctx.rearrange("(r b) (p g c) d -> r g p b (c d)", b=2, g=GROUPS, c=PER_GROUP)

    es = ExitStack()
    with es:
        def sb(name, shape, dt=fp32):
            return es.enter_context(nc.sbuf_tensor(name, shape, dt))

        def sem(name):
            return es.enter_context(nc.semaphore(name))

        def before(name, shape, later):
            with nc.sbuf_tensor(name, shape, fp32) as first:
                pass
            left = int(np.prod(shape[1:]))
            seconds = []
            for part, n, dt in later:
                seconds.append(sb(part, [P, n], dt))
                left -= n
            assert left >= 0
            if left:
                sb(f"{name}_rest", [P, left])
            return first, seconds

        ctx_cols, (slot0, slot1, slot2, down_hi2, down_lo2) = before("ctx_cols", [P, KD * 2 * CTX], (
            ("slot0", WFREE, fp32), ("slot1", WFREE, fp32), ("slot2", WFREE, fp32),
            ("down_hi2", DOWN, f32r), ("down_lo2", DOWN, f32r)))
        ctx_rows, split_parts = before("ctx_rows", [P, GROUPS, 2, PER_GROUP * DIM], (
            ("up_hi0", UP, f32r), ("up_lo0", UP, f32r), ("up_hi1", UP, f32r), ("up_lo1", UP, f32r),
            ("down_hi0", DOWN, f32r), ("down_lo0", DOWN, f32r), ("down_hi1", DOWN, f32r), ("down_lo1", DOWN, f32r)))
        w_qk, (slot3, down_hi3) = before("w_qk", [P, 2 * KD * DIM], (("slot3", WFREE, fp32), ("down_hi3", DOWN, f32r)))
        down_lo3 = sb("down_lo3", [P, DOWN], f32r)
        xs = sb("xs", [P, PAIRS, DIM])
        w_fold = sb("w_fold", [P, KD, DIM])
        fold_cols = sb("fold_cols", [P, 2 * KD + 1])
        shared_sb = sb("shared_sb", [P, WFREE])
        gate_sb = sb("gate_sb", [P, KD, EXPERTS])
        gate_bias = sb("gate_bias", [P, EXPERTS])
        bq_sb = sb("bq_sb", [P, KD])
        bk_sb = sb("bk_sb", [P, KD])
        cst = sb("cst", [P, C_ALL])
        tri = sb("tri", [P, P], bf16)
        ones = sb("ones", [P, P], bf16)
        zero_rows = sb("zero_rows", [P, DIM])
        neg_half = sb("neg_half", [P, 1])
        xn = sb("xn", [P, DIM])
        xn_t = sb("xn_t", [P, KD, P])
        g_t = sb("g_t", [P, KD, P])
        probs = sb("probs", [P, CTX])
        probs_t, (y_sb,) = before("probs_t", [P, ROW_TILES * P], (("y_sb", 2 * DIM, fp32),))
        h = sb("h", [P, DIM])
        h_t = sb("h_t", [P, KD, P])
        acc = sb("acc", [P, DIM])
        tanh_half = sb("tanh_half", [P, KI, P])
        gated = sb("gated", [P, KI, P])
        z = sb("z", [P, KI, P])
        stats = sb("stats", [P, 6])
        mean_var = sb("mean_var", [P, 2])
        var_eps = sb("var_eps", [P, 1])
        rstd = sb("rstd", [P, 1])
        row_max = sb("row_max", [P, 1])
        max_c = sb("max_c", [P, 1])
        exp_bias = sb("exp_bias", [P, 1])
        row_sum = sb("row_sum", [P, 1])
        row_inv = sb("row_inv", [P, 1])
        c_sb = sb("c_sb", [P, 1])
        g_exp = sb("g_exp", [P, EXPERTS])
        g_exp1 = sb("g_exp1", [P, EXPERTS])
        g_sig = sb("g_sig", [P, EXPERTS])
        g_score = sb("g_score", [P, EXPERTS])
        top = sb("top", [P, 8])
        top_i = sb("top_i", [P, 8], u32)
        top_f = sb("top_f", [P, TOPK])
        w_sum = sb("w_sum", [P, 1])
        w_inv = sb("w_inv", [P, 1])
        onehot = sb("onehot", [P, TOPK, EXPERTS])
        picked = sb("picked", [P, EXPERTS])
        mask = sb("mask", [P, EXPERTS], bf16)
        base = sb("base", [P, EXPERTS])
        rank = sb("rank", [P, EXPERTS])
        rank_sel = sb("rank_sel", [P, TOPK, EXPERTS])
        place_f = sb("place_f", [P, TOPK])
        place = sb("place", [P, TOPK], i32)
        dump_at = sb("dump_at", [P, TOPK])
        token = sb("token", [P, 1])
        entry = sb("entry", [P, TOPK, 2], i32)
        cnt = sb("cnt", [1, EXPERTS])
        above = sb("above", [1, EXPERTS, TILES_MAX])
        n_tiles = sb("n_tiles", [1, EXPERTS])
        active = sb("active", [1, EXPERTS])
        incl = sb("incl", [1, EXPERTS])
        excl = sb("excl", [1, EXPERTS])
        turn = sb("turn", [1, EXPERTS, EXPERTS])
        turn_on = sb("turn_on", [1, EXPERTS, EXPERTS])
        turn_n = sb("turn_n", [1, EXPERTS, EXPERTS])
        turn_e = sb("turn_e", [1, EXPERTS, EXPERTS])
        plan_f = sb("plan_f", [1, 2 * EXPERTS + 4])
        plan = sb("plan", [1, 2 * EXPERTS + 4], i32)
        ring = sb("ring", [P, RING, 2], i32)
        take_at = sb("take_at", [P, 1], i32)
        add_at = sb("add_at", [P, 1], i32)
        taken = sb("taken", [P, HELD, DIM])
        taken_now = sb("taken_now", [P, DIM])
        taken_hi = sb("taken_hi", [P, KD, P], f32r)
        taken_lo = sb("taken_lo", [P, KD, P], f32r)
        half_tanh = sb("half_tanh", [P, INNER])
        gated_rows = sb("gated_rows", [P, INNER])
        z_rows = sb("z_rows", [P, INNER])
        zt_hi = sb("zt_hi", [P, KI, P], f32r)
        zt_lo = sb("zt_lo", [P, KI, P], f32r)

        ident = cst[:, C_ID:C_ID + P]
        iota16 = cst[:, C_IOTA:C_IOTA + EXPERTS]
        region = cst[:, C_REGION:C_REGION + EXPERTS]
        valid = cst[:, C_VALID:C_VALID + 1]

        scores = es.enter_context(nc.psum_tensor("scores", [P, CHUNKS, 512], fp32))
        b3, b4, b5, b6, b7 = (es.enter_context(nc.psum_tensor(n, [P, 512], fp32))
                              for n in ("b3", "b4", "b5", "b6", "b7"))

        x_loaded, c_loaded = sem("x_loaded"), sem("c_loaded")
        wq_loaded, wk_loaded, sh_loaded = sem("wq_loaded"), sem("wk_loaded"), sem("sh_loaded")
        cols_loaded = [sem(f"cols_loaded{k}") for k in range(KD)]
        rows_loaded = [sem(f"rows_loaded{g}") for g in range(GROUPS)]
        cols_used, rows_used = sem("cols_used"), sem("rows_used")
        init_ready, init_stored = sem("init_ready"), sem("init_stored")
        var_ready, rstd_ready, xn_ready = sem("var_ready"), sem("rstd_ready"), sem("xn_ready")
        xt_ready, xnt_ready = sem("xt_ready"), sem("xnt_ready")
        fold_ready, folded, g_ready, gt_ready, c_read = (sem("fold_ready"), sem("folded"), sem("g_ready"),
                                                         sem("gt_ready"), sem("c_read"))
        bias_ready, probs_ready = sem("bias_ready"), sem("probs_ready")
        pt_ready, ptt_ready = sem("pt_ready"), sem("ptt_ready")
        x1_ready, h_ready, ht_ready, htt_ready = sem("x1_ready"), sem("h_ready"), sem("ht_ready"), sem("htt_ready")
        gate_ready, gexp_ready, mask_ready = sem("gate_ready"), sem("gexp_ready"), sem("mask_ready")
        rank_ready, rank_read, entries_ready = sem("rank_ready"), sem("rank_read"), sem("entries_ready")
        entries_stored, h_stored, acc_stored = sem("entries_stored"), sem("h_stored"), sem("acc_stored")
        up_ready, tanh_ready, z_ready, y_ready, acc_ready = (sem("up_ready"), sem("tanh_ready"), sem("z_ready"),
                                                             sem("y_ready"), sem("acc_ready"))
        plan_ready, entry_free = sem("plan_ready"), sem("entry_free")
        entry_loaded = [sem(f"entry_loaded{i}") for i in range(2)]
        expert_loaded = [sem(f"expert_loaded{i}") for i in range(SLOTS)]
        gathered, now_ready, taken_used = sem("gathered"), sem("now_ready"), sem("taken_used")
        guess_loaded = sem("guess_loaded")
        hi_ready, lo_ready = sem("hi_ready"), sem("lo_ready")
        gu_ready, half_ready, gated_ready, z_rows_ready = (sem(n) for n in ("gu_ready", "half_ready", "gated_ready",
                                                                           "z_rows_ready"))
        taken_hi_ready, taken_lo_ready = sem("taken_hi_ready"), sem("taken_lo_ready")
        zt_ready, zt_hi_ready, zt_lo_ready = sem("zt_ready"), sem("zt_hi_ready"), sem("zt_lo_ready")
        ysb_ready, added = sem("ysb_ready"), sem("added")
        folded_half = sem("folded_half")
        waited = sem("waited")
        dve_step, pool_step = sem("dve_step"), sem("pool_step")

        block = es.enter_context(nc.Block())

        def settle(eng):
            eng.sem_inc(waited, 1)

        wq_sb = w_qk[:, 0:KD * DIM].rearrange("p (k n) -> p k n", k=KD)
        wk_sb = w_qk[:, KD * DIM:].rearrange("p (k n) -> p k n", k=KD)

        class Turns:

            def __init__(self, eng, name):
                self.eng = eng
                self.tile, self.now, self.next = (eng.alloc_register(f"{name}_{r}") for r in ("tile", "now", "next"))
                eng.reg_mov(self.tile, 0)
                eng.reg_mov(self.now, self.load(0))
                eng.reg_mov(self.next, self.load(1))

            def load(self, turn):
                return self.eng.value_load(plan[0:1, bass.ds(turn, 1)], min_val=0, max_val=TILES_MAX)

            def count(self, reg):
                return self.eng.snap(reg, min_val=0, max_val=TILES_MAX)

            def t(self, first=0):
                return self.eng.snap(self.tile, min_val=first, max_val=EXPERTS * TILES_MAX)

        expert_w = [slot0[:, :], slot1[:, :], slot2[:, :], slot3[:, :]]
        up_parts = [split_parts[0:2], split_parts[2:4]]
        down_parts = [split_parts[4:6], split_parts[6:8], [down_hi2, down_lo2], [down_hi3, down_lo3]]

        def piece(s, i):
            if i < KD:
                at = slice(i * 2 * INNER, (i + 1) * 2 * INNER)
                return expert_w[s][:, at], [part[:, at] for part in up_parts[s % 2]]
            at = slice((i - KD) * DIM, (i - KD + 1) * DIM)
            return expert_w[s][:, UP + at.start:UP + at.stop], [part[:, at] for part in down_parts[s]]

        @block.sync
        def _(sp):
            for i in range(2):
                sp.sem_inc(entry_loaded[i], 16)
            sp.dma_start(cst[:], consts).then_inc(c_loaded, 16)
            sp.dma_start(wq_sb, wq).then_inc(wq_loaded, 16)
            sp.dma_start(wk_sb, wk).then_inc(wk_loaded, 16)
            sp.dma_start(bq_sb[:], bq).then_inc(wq_loaded, 16)
            sp.dma_start(bk_sb[:], bk).then_inc(wk_loaded, 16)
            for b in range(2):
                sp.dma_start(xs[HALF * b:HALF * b + TEXT, :, :], x_v[b]).then_inc(x_loaded, 16)
            for b in range(2):
                sp.dma_start(xs[HALF * b + TEXT:HALF * (b + 1), :, :], entry_init[1]).then_inc(x_loaded, 16)

            def load_cols(r, k):
                sp.dma_start(ctx_cols[:, k * 2 * CTX:(k + 1) * 2 * CTX],
                             ctx_t[bass.ds(r, 1), k, :, :].rearrange("a p n -> (a p) n")).then_inc(cols_loaded[k], 16)

            def load_rows(r, g):
                v = nat_v[bass.ds(r, 1), g, :, :, :].rearrange("a p b n -> (a p) b n")
                sp.dma_start(ctx_rows[0:SPRAY, g, :, :], v[0:SPRAY]).then_inc(rows_loaded[g], 16)
                sp.dma_start(ctx_rows[SPRAY:ROW_TILE, g, :, :], v[SPRAY:ROW_TILE]).then_inc(rows_loaded[g], 16)

            for k in range(KD):
                load_cols(0, k)
            for g in range(GROUPS):
                load_rows(0, g)
            sp.dma_start(gate_sb[:], gate_t).then_inc(sh_loaded, 16)
            sp.dma_start(gate_bias[:], gate_b.to_broadcast([P, EXPERTS])).then_inc(sh_loaded, 16)
            sp.dma_start(shared_sb[:], shared).then_inc(sh_loaded, 16)
            sp.wait_ge(init_ready, 1)
            sp.dma_start(h_rows[TOKENS:TOKENS + P, :], zero_rows[:]).then_inc(init_stored, 16)

            with sp.Fori(0, PAIRS - 1) as r:
                for k in range(KD):
                    sp.wait_ge(cols_used, r * KD + (k + 1))
                    load_cols(r + 1, k)
                for g in range(GROUPS):
                    sp.wait_ge(rows_used, r * GROUPS + (g + 1))
                    load_rows(r + 1, g)

            def load_weights(s, e):
                src = experts[e] if isinstance(e, int) else experts[bass.ds(e, 1), :, :].rearrange("a p n -> (a p) n")
                sp.dma_start(expert_w[s], src).then_inc(expert_loaded[s], 16)
                settle(sp)

            def load_entries(e, j):
                tv = sp.snap(t, min_val=0, max_val=EXPERTS * TILES_MAX)
                slot, at = sp.snap(tv % RING), sp.snap((e * (REGION // P) + j) * P)
                sp.wait_ge(entry_free, sp.snap(tv + 1))
                settle(sp)
                parity = sp.snap(tv % 2)
                for i in range(2):
                    with (sp.If(parity > 0) if i else sp.If(parity < 1)):
                        sp.wait_ge(entry_loaded[i], sp.snap((tv // 2 + 1) * 16))
                        settle(sp)
                        sp.dma_start(ring[:, bass.ds(slot, 1), :].rearrange("p a c -> p (a c)"),
                                     entries[bass.ds(at, P), :]).then_inc(entry_loaded[i], 16)
                sp.reg_add(t, t, 1)

            sp.wait_ge(cols_used, KD * PAIRS)
            load_weights(0, 0)
            sp.dma_start(expert_w[1], experts[1]).then_inc(guess_loaded, 16)
            sp.wait_ge(plan_ready, 1)
            sp.wait_ge(guess_loaded, 16)
            second = sp.value_load(plan[0:1, EXPERTS + 3:EXPERTS + 4], min_val=0, max_val=EXPERTS - 1)
            with sp.If(second > 1):
                load_weights(1, second)
            with sp.If(second < 2):
                sp.sem_inc(expert_loaded[1], 16)
            t = sp.alloc_register("sp_tile")
            sp.reg_mov(t, 0)
            with sp.Fori(0, EXPERTS // SLOTS) as lap:
                for s in range(SLOTS):
                    n = sp.value_load(plan[0:1, bass.ds(lap * SLOTS + s, 1)], min_val=0, max_val=TILES_MAX)
                    e = sp.value_load(plan[0:1, bass.ds(lap * SLOTS + (EXPERTS + 2 + s), 1)], min_val=0,
                                      max_val=EXPERTS - 1)
                    with sp.If(n > 0):
                        if s == 0:
                            sp.wait_ge(entries_stored, (PAIRS * TOPK + 1) * 16)
                        with sp.Fori(0, n) as j:
                            load_entries(e, j)

                        def load_next():
                            with sp.If(sp.value_load(plan[0:1, bass.ds(lap * SLOTS + (s + 1), 1)], min_val=0,
                                                     max_val=TILES_MAX) > 0):
                                sp.wait_ge(lo_ready, lap * (SLOTS * PIECES) + (s + 2) * PIECES)
                                settle(sp)
                                load_weights((s + 1) % SLOTS, sp.value_load(
                                    plan[0:1, bass.ds(lap * SLOTS + (EXPERTS + 3 + s), 1)], min_val=0,
                                    max_val=EXPERTS - 1))
                        if s == 0:
                            with sp.If(lap > 0):
                                load_next()
                        else:
                            load_next()

        @block.gpsimd
        def _(pool):
            nc.gpsimd.memset(neg_half[:], -0.5).then_inc(pool_step, 1)
            nc.gpsimd.memset(zero_rows[:], 0.0).then_inc(init_ready, 1)
            pool.sem_inc(entry_free, RING)
            pool.wait_ge(pool_step, 1)

            pool.wait_ge(init_ready, 1)
            pool.dma_start(entries[0:DUMP, :].rearrange("(p n) c -> p (n c)", p=P), entry_init[0]
                           ).then_inc(entries_stored, 16)
            for i in range(2):
                pool.dma_start(out[TOKENS + i * HALF:TOKENS + (i + 1) * HALF, :], zero_rows[0:HALF, :]
                               ).then_inc(added, 16)

            def power(i):
                pool.wait_ge(var_ready, i + 1)
                nc.gpsimd.tensor_tensor(rstd[:], var_eps[:], neg_half[:], ALU.pow).then_inc(rstd_ready, 1)

            def scatter(r):
                pool.wait_ge(entries_ready, r + 1)
                settle(pool)
                for k in range(TOPK):
                    nc.gpsimd.indirect_dma_start(
                        entries[:, :], bass.IndirectOffsetOnAxis(ap=place[:, k:k + 1], axis=0),
                        entry[:, k, :], None).then_inc(entries_stored, 16)

            power(0)
            power(1)
            pool.wait_ge(entries_stored, 16)
            with pool.Fori(1, PAIRS - 1) as p:
                power(p * 2)
                power(p * 2 + 1)
                scatter(p - 1)
            power(2 * PAIRS - 2)
            scatter(PAIRS - 2)
            power(2 * PAIRS - 1)
            scatter(PAIRS - 1)

            pool.wait_ge(plan_ready, 1)
            lead = pool.value_load(plan[0:1, 2 * EXPERTS + 3:2 * EXPERTS + 4], min_val=TOKENS * TOPK // P - AHEAD,
                                   max_val=TOKENS * TOPK // P + EXPERTS)
            pool.wait_ge(init_stored, 16)
            pool.wait_ge(h_stored, PAIRS * 32 + 16)

            def gather(t):
                pool.wait_ge(entry_loaded[0], (t // 2 + 2) * 16)
                settle(pool)
                pool.wait_ge(entry_loaded[1], ((t + 1) // 2 + 1) * 16)
                nc.gpsimd.tensor_copy(take_at[:], ring[:, bass.ds(t % RING, 1), 0]).then_inc(pool_step, 1)

            def one_of(t, count, start):
                if isinstance(t, int):
                    start(t % count)
                    return
                at = pool.snap(t % count)
                for i in range(count):
                    with pool.If(at > i - 1):
                        with pool.If(at < i + 1):
                            start(i)

            def gather_start(t):
                if not isinstance(t, int) or t >= HELD:
                    pool.wait_ge(now_ready, t - (HELD - 1))
                settle(pool)
                one_of(t, HELD, lambda i: nc.gpsimd.indirect_dma_start(
                    taken[:, i, :], None, h_rows[:, :], bass.IndirectOffsetOnAxis(ap=take_at[:, 0:1], axis=0)
                    ).then_inc(gathered, 16))

            def add(t):
                pool.wait_ge(added, (t + 2) * 16)
                settle(pool)
                one_of(t, 2, lambda i: nc.gpsimd.indirect_dma_start(
                    out[:, :], bass.IndirectOffsetOnAxis(ap=add_at[:, 0:1], axis=0),
                    y_sb[:, i * DIM:(i + 1) * DIM], None, compute_op=ALU.add).then_inc(added, 16))

            def add_index(t):
                nc.gpsimd.tensor_copy(add_at[:], ring[:, bass.ds(t % RING, 1), 0]).then_inc(entry_free, 1)

            def take(t):
                pool.wait_ge(gathered, t * 16)
                gather(t)
                pool.wait_ge(pool_step, t + 2)
                gather_start(t)

            def give(t):
                pool.wait_ge(added, (t + 2) * 16)
                pool.wait_ge(ysb_ready, t + 2)
                add_index(t)
                pool.wait_ge(entry_free, t + (RING + 1))
                add(t)

            for i in range(AHEAD):
                take(i)
            pool.wait_ge(acc_stored, PAIRS * 32 + 16)
            with pool.Fori(0, lead) as t:
                take(t + AHEAD)
                give(t)
            for i in range(AHEAD):
                if i < 2:
                    pool.wait_ge(gathered, (lead + (AHEAD + i)) * 16)
                    gather_start(lead + (AHEAD + i))
                give(lead + i)
            pool.wait_ge(added, (lead + (AHEAD + 2)) * 16)
            pool.wait_ge(gathered, (lead + (AHEAD + 2)) * 16)

        @block.tensor
        def _(pe):
            def transposes(bank, src):
                for k in range(KD):
                    last = nc.tensor.transpose(bank[:, k * P:(k + 1) * P], src[:, k * P:(k + 1) * P], ident)
                return last

            def x_transpose(p, bank):
                pe.wait_ge(xn_ready, p + 1)
                transposes(bank, xn).then_inc(xt_ready, 1)

            def fold():
                pe.wait_ge(wq_loaded, 32)
                pe.wait_ge(wk_loaded, 32)
                for m, bank in enumerate((scores[:, 0, :], scores[:, 1, :], scores[:, 2, :], b6[:, :])):
                    for k in range(KD):
                        last = nc.tensor.matmul(bank, wq_sb[:, k, m * P:(m + 1) * P], wk_sb[:, k, :],
                                                start=(k == 0), stop=(k == KD - 1))
                    last.then_inc(fold_ready, 1)
                for col in range(2 * KD):
                    w, vec = ((wk_sb, bq_sb), (wq_sb, bk_sb))[col // KD]
                    at = col % KD * P
                    for k in range(KD):
                        nc.tensor.matmul(b7[:, col:col + 1], w[:, k, at:at + P], vec[:, k:k + 1],
                                         start=(k == 0), stop=(k == KD - 1))
                for k in range(KD):
                    last = nc.tensor.matmul(b7[:, 2 * KD:2 * KD + 1], bq_sb[:, k:k + 1].to_broadcast([P, P]),
                                            bk_sb[:, k:k + 1], start=(k == 0), stop=(k == KD - 1))
                last.then_inc(fold_ready, 1)

            def project(p):
                pe.wait_ge(xnt_ready, p + 1)
                for m in range(KD):
                    for k in range(KD):
                        last = nc.tensor.matmul(b7[:, m * P:(m + 1) * P], w_fold[:, k, m * P:(m + 1) * P],
                                                xn_t[:, k, :], start=(k == 0), stop=(k == KD - 1))
                last.then_inc(g_ready, 1)

            def project_bias(p):
                for k in range(KD):
                    last = nc.tensor.matmul(b3[:, 32:33], xn_t[:, k, :], fold_cols[:, KD + k:KD + k + 1],
                                            start=(k == 0), stop=(k == KD - 1))
                last.then_inc(g_ready, 1)

            def score(p):
                pe.wait_ge(gt_ready, p + 1)
                pe.wait_ge(probs_ready, p)
                for k in range(KD):
                    pe.wait_ge(cols_loaded[k], (p + 1) * 16)
                    for n in range(CHUNKS):
                        for b in range(2):
                            at = (2 * k + b) * CTX + n * CHUNK
                            last = nc.tensor.matmul(scores[HALF * b:HALF * (b + 1), n, 0:CHUNK],
                                                    g_t[:, k, HALF * b:HALF * (b + 1)],
                                                    ctx_cols[:, at:at + CHUNK],
                                                    start=(k == 0), stop=(k == KD - 1))
                    last.then_inc(cols_used, 1)

            def transpose_probs(p, g):
                bank = (b4, b5)[g % 2]
                if g == 0:
                    pe.wait_ge(probs_ready, p + 1)
                if g == 2:
                    pe.wait_ge(ptt_ready, p * GROUPS + 1)
                for c in range(PER_GROUP):
                    at = (g * PER_GROUP + c) * ROW_TILE
                    last = nc.tensor.transpose(bank[0:ROW_TILE, c * P:(c + 1) * P],
                                               probs[:, at:at + ROW_TILE], ident)
                last.then_inc(pt_ready, 1)

            def attend(p):
                for g in range(GROUPS):
                    pe.wait_ge(ptt_ready, p * GROUPS + (g + 1))
                    pe.wait_ge(rows_loaded[g], (p + 1) * 32)
                    for c in range(PER_GROUP):
                        for b in range(2):
                            at = (g * PER_GROUP + c) * P + HALF * b
                            first, end = g + c == 0, g * PER_GROUP + c == ROW_TILES - 1
                            last = nc.tensor.matmul(b3[HALF * b:HALF * (b + 1), :],
                                                    probs_t[0:ROW_TILE, at:at + HALF],
                                                    ctx_rows[0:ROW_TILE, g, b, c * DIM:(c + 1) * DIM],
                                                    start=first, stop=end)
                    last.then_inc(rows_used, 1)

            def h_transpose(r):
                pe.wait_ge(h_ready, r + 1)
                transposes(b4, h).then_inc(ht_ready, 1)

            def gate(r):
                pe.wait_ge(htt_ready, r + 1)
                for k in range(KD):
                    last = nc.tensor.matmul(b3[:, 0:EXPERTS], h_t[:, k, :], gate_sb[:, k, :],
                                            start=(k == 0), stop=(k == KD - 1))
                last.then_inc(gate_ready, 1)

            def ranks(r):
                pe.wait_ge(mask_ready, r + 1)
                nc.tensor.matmul(scores[:, 0, 0:EXPERTS], tri[:], mask[:], start=True, stop=True)
                nc.tensor.matmul(scores[:, 0, EXPERTS:2 * EXPERTS], ones[:], mask[:], start=True, stop=True
                                 ).then_inc(rank_ready, 1)

            def up(w, src_t):
                for i in range(KI):
                    bank = (b6, b7)[i]
                    for half in range(2):
                        for k in range(KD):
                            at = (2 * k + half) * INNER + i * P
                            last = nc.tensor.matmul(bank[:, half * P:(half + 1) * P], w[:, at:at + P],
                                                    src_t[:, k, :], start=(k == 0), stop=(k == KD - 1))
                    last.then_inc(up_ready, 1)

            def down(w, uses):
                for i in range(KI):
                    pe.wait_ge(z_ready, uses * KI + (i + 1))
                    at = KD * 2 * INNER + i * DIM
                    last = nc.tensor.matmul(b3[:, :], z[:, i, :], w[:, at:at + DIM],
                                            start=(i == 0), stop=(i == KI - 1))
                last.then_inc(y_ready, 1)

            pe.sem_inc(ht_ready, 1)
            fold()
            pe.wait_ge(c_loaded, 16)
            x_transpose(0, b5)
            pe.wait_ge(folded, 1)
            project(0)
            project_bias(0)
            score(0)
            x_transpose(1, b5)
            pe.wait_ge(gt_ready, 1)
            project(1)
            pe.wait_ge(c_read, 1)
            project_bias(1)
            for g in range(GROUPS):
                transpose_probs(0, g)
            pe.wait_ge(sh_loaded, 48)
            pe.wait_ge(c_read, 2)
            attend(0)
            with pe.Fori(1, PAIRS - 1) as p:
                score(p)
                h_transpose(p - 1)
                x_transpose(p + 1, b5)
                gate(p - 1)
                project(p + 1)
                pe.wait_ge(gexp_ready, p)
                project_bias(p + 1)
                pe.wait_ge(gt_ready, p + 2)
                up(shared_sb, h_t)
                pe.wait_ge(probs_ready, p + 1)
                ranks(p - 1)
                transpose_probs(p, 0)
                transpose_probs(p, 1)
                pe.wait_ge(c_read, p + 2)
                down(shared_sb, p - 1)
                transpose_probs(p, 2)
                pe.wait_ge(acc_ready, p)
                attend(p)
                pe.wait_ge(rank_read, p)
            last_pair = PAIRS - 1
            score(last_pair)
            h_transpose(last_pair - 1)
            gate(last_pair - 1)
            up(shared_sb, h_t)
            pe.wait_ge(probs_ready, PAIRS)
            ranks(last_pair - 1)
            transpose_probs(last_pair, 0)
            transpose_probs(last_pair, 1)
            transpose_probs(last_pair, 2)
            pe.wait_ge(gexp_ready, last_pair)
            attend(last_pair)
            pe.wait_ge(x1_ready, PAIRS)
            down(shared_sb, last_pair - 1)
            h_transpose(last_pair)
            pe.wait_ge(acc_ready, last_pair)
            gate(last_pair)
            pe.wait_ge(rank_read, last_pair)
            ranks(last_pair)
            up(shared_sb, h_t)
            pe.wait_ge(gexp_ready, PAIRS)
            down(shared_sb, last_pair)

            def tile_transpose(t):
                pe.wait_ge(now_ready, t + 1)
                transposes(b4, taken_now).then_inc(taken_used, 1)

            def three(bank, n, hi, w_hi, w_lo, blocks, lo, parts_ready, t):
                def part(a, w, k, start=False, stop=False):
                    return nc.tensor.matmul(bank[:, :], a[:, k, :], w[:, k * n:(k + 1) * n], start=start, stop=stop)
                for k in range(blocks):
                    part(hi, w_hi, k, start=(k == 0))
                    part(hi, w_lo, k)
                pe.wait_ge(parts_ready, t)
                settle(pe)
                for k in range(blocks):
                    last = part(lo, w_hi, k, stop=(k == blocks - 1))
                return last

            def tile_up(t, s):
                pe.wait_ge(taken_hi_ready, t + 1)
                settle(pe)
                three(b6, 2 * INNER, taken_hi, *up_parts[s % 2], KD, taken_lo, taken_lo_ready, t + 1
                      ).then_inc(gu_ready, 1)

            def tile_down(t, s):
                pe.wait_ge(zt_hi_ready, t)
                settle(pe)
                pe.wait_ge(ysb_ready, t)
                settle(pe)
                three(b3, DIM, zt_hi, *down_parts[s], KI, zt_lo, zt_lo_ready, t).then_inc(y_ready, 1)

            def z_transpose(t):
                pe.wait_ge(z_rows_ready, t)
                settle(pe)
                for i in range(KI):
                    last = nc.tensor.transpose(b5[:, i * P:(i + 1) * P], z_rows[:, i * P:(i + 1) * P], ident)
                last.then_inc(zt_ready, 1)

            pe.wait_ge(plan_ready, 1)
            turns = Turns(pe, "pe")
            slot = pe.alloc_register("pe_slot")
            pe.reg_mov(slot, 0)
            tile_transpose(0)
            pe.wait_ge(acc_ready, PAIRS)
            with pe.Fori(0, EXPERTS // SLOTS) as lap:
                for s in range(SLOTS):
                    with pe.If(turns.count(turns.now) > 0):
                        tv = turns.t()
                        if s == 0:
                            with pe.If(tv > 0):
                                z_transpose(turns.t(1))
                        else:
                            z_transpose(tv)
                        pe.wait_ge(lo_ready, lap * (SLOTS * PIECES) + (SLOTS * PIECES + s * PIECES + KD))
                        settle(pe)
                        tile_up(tv, s)
                        later = turns.load(lap * SLOTS + (s + 2))
                        tile_transpose(tv + 1)
                        if s == 0:
                            with pe.If(tv > 0):
                                tile_down(turns.t(1), SLOTS - 1)
                        else:
                            tile_down(tv, s - 1)
                        pe.reg_add(turns.tile, turns.tile, 1)
                        with pe.If(turns.count(turns.now) > 1):
                            pe.wait_ge(lo_ready, lap * (SLOTS * PIECES) + (SLOTS * PIECES + (s + 1) * PIECES))
                            settle(pe)
                            with pe.Fori(1, turns.count(turns.now)) as j:
                                tv = turns.t(1)
                                z_transpose(tv)
                                tile_up(tv, s)
                                tile_transpose(tv + 1)
                                tile_down(tv, s)
                                pe.reg_add(turns.tile, turns.tile, 1)
                        pe.reg_mov(slot, s)
                        pe.reg_mov(turns.now, turns.next)
                        pe.reg_mov(turns.next, later)
            z_transpose(turns.t(1))
            last = pe.snap(slot, min_val=0, max_val=SLOTS - 1)
            for s in range(SLOTS):
                with pe.If(last > s - 1):
                    with pe.If(last < s + 1):
                        tile_down(turns.t(1), s)

        @block.scalar
        def _(act):
            def copy_x_t(p, bank):
                act.wait_ge(xt_ready, p + 1)
                nc.scalar.copy(xn_t[:].rearrange("p k n -> p (k n)"), bank[:, :]).then_inc(xnt_ready, 1)

            def softmax(p):
                act.wait_ge(bias_ready, p + 1)
                nc.scalar.activation(probs[:].rearrange("p (n c) -> p n c", n=CHUNKS), scores[:, :, 0:CHUNK],
                                     ACT.Exp, bias=exp_bias[:], scale=SCALE, accum_out=row_sum[:]
                                     ).then_inc(probs_ready, 1)

            def copy_probs_t(p):
                for g in range(GROUPS):
                    act.wait_ge(pt_ready, p * GROUPS + (g + 1))
                    nc.scalar.copy(probs_t[0:ROW_TILE, g * PER_GROUP * P:(g + 1) * PER_GROUP * P],
                                   (b4, b5)[g % 2][0:ROW_TILE, :]).then_inc(ptt_ready, 1)

            def copy_h_t(r):
                act.wait_ge(ht_ready, r + 2)
                nc.scalar.copy(h_t[:].rearrange("p k n -> p (k n)"), b4[:, :]).then_inc(htt_ready, 1)

            def store_pair(r, src, dst, done):
                for b in range(2):
                    act.dma_start(dst[bass.ds(r * PAIR_TOKENS + b * TEXT, TEXT), :],
                                  src[HALF * b:HALF * b + TEXT, :]).then_inc(done, 16)

            def gate_exp(r):
                act.wait_ge(gate_ready, r + 1)
                nc.scalar.activation(g_exp[:], b3[:, 0:EXPERTS], ACT.Exp, scale=-1.0).then_inc(gexp_ready, 1)

            def up_tanh(uses):
                for i in range(KI):
                    act.wait_ge(up_ready, uses * KI + (i + 1))
                    nc.scalar.activation(tanh_half[:, i, :], (b6, b7)[i][:, 0:P], ACT.Tanh, scale=0.5
                                         ).then_inc(tanh_ready, 1)

            def split_hi(s, blocks):
                for i in blocks:
                    src, (hi, _) = piece(s, i)
                    nc.scalar.copy(hi, src).then_inc(hi_ready, 1)

            for done, n in ((h_stored, 16), (acc_stored, 16), (ysb_ready, 1)):
                act.sem_inc(done, n)
            for m in range(2):
                act.wait_ge(fold_ready, m + 1)
                nc.scalar.copy(w_fold[:, m, :], scores[:, m, :]).then_inc(folded_half, 1)
            copy_x_t(0, b5)
            copy_x_t(1, b5)
            softmax(0)
            copy_probs_t(0)
            with act.Fori(1, PAIRS - 1) as p:
                act.wait_ge(h_ready, p)
                store_pair(p - 1, h, h_rows, h_stored)
                copy_h_t(p - 1)
                copy_x_t(p + 1, b5)
                gate_exp(p - 1)
                softmax(p)
                up_tanh(p - 1)
                copy_probs_t(p)
                act.wait_ge(acc_ready, p)
                store_pair(p - 1, acc, out, acc_stored)
            last_pair = PAIRS - 1
            act.wait_ge(h_ready, last_pair)
            store_pair(last_pair - 1, h, h_rows, h_stored)
            copy_h_t(last_pair - 1)
            gate_exp(last_pair - 1)
            softmax(last_pair)
            up_tanh(last_pair - 1)
            copy_probs_t(last_pair)
            act.wait_ge(h_ready, PAIRS)
            store_pair(last_pair, h, h_rows, h_stored)
            copy_h_t(last_pair)
            act.wait_ge(acc_ready, last_pair)
            store_pair(last_pair - 1, acc, out, acc_stored)
            gate_exp(last_pair)
            act.wait_ge(rows_used, GROUPS * PAIRS)
            act.wait_ge(expert_loaded[0], 16)
            split_hi(0, range(PIECES))
            up_tanh(last_pair)
            act.wait_ge(acc_ready, PAIRS)
            store_pair(last_pair, acc, out, acc_stored)

            def copy_taken(t):
                act.wait_ge(gathered, (t + 1) * 16)
                if not isinstance(t, int) or t > 0:
                    act.wait_ge(taken_used, t)
                nc.scalar.copy(taken_now[:], taken[:, bass.ds(t % HELD, 1), :].rearrange("p a n -> p (a n)")
                                      ).then_inc(now_ready, 1)

            def taken_to_hi(t):
                act.wait_ge(taken_used, t + 1)
                settle(act)
                nc.scalar.copy(taken_hi[:].rearrange("p k n -> p (k n)"), b4[:, :]).then_inc(taken_hi_ready, 1)

            def weigh(t):
                act.wait_ge(y_ready, t + PAIRS)
                act.wait_ge(added, t * 16)
                act.wait_ge(entry_loaded[0], ((t + 1) // 2 + 1) * 16)
                settle(act)
                act.wait_ge(entry_loaded[1], (t // 2 + 1) * 16)
                nc.scalar.activation(y_sb[:, bass.ds((t + 1) % 2 * DIM, DIM)], b3[:, :], ACT.Copy,
                                     scale=ring[:, bass.ds((t + (RING - 1)) % RING, 1), 1].bitcast(fp32)
                                     ).then_inc(ysb_ready, 1)

            def tile(first=False, turn=None):
                tv = turns.t(0 if first else 1)
                act.wait_ge(gu_ready, tv + 1)
                settle(act)
                nc.scalar.activation(half_tanh[:], b6[:, 0:INNER], ACT.Tanh, scale=0.5).then_inc(half_ready, 1)
                taken_to_hi(tv + 1)
                copy_taken(tv + 2)
                later = None if turn is None else turns.load(turn)
                if first:
                    with act.If(tv > 0):
                        weigh(turns.t(1))
                else:
                    weigh(tv)
                act.wait_ge(zt_ready, tv + 1)
                settle(act)
                nc.scalar.copy(zt_hi[:].rearrange("p k n -> p (k n)"), b5[:, 0:INNER]).then_inc(zt_hi_ready, 1)
                act.reg_add(turns.tile, turns.tile, 1)
                return later

            act.wait_ge(plan_ready, 1)
            copy_taken(0)
            taken_to_hi(0)
            copy_taken(1)
            turns = Turns(act, "act")
            with act.Fori(0, EXPERTS // SLOTS) as lap:
                for s in range(SLOTS):
                    after = (s + 1) % SLOTS
                    with act.If(turns.count(turns.now) > 0):
                        n, more = turns.count(turns.now), turns.count(turns.next)
                        with act.If(more > 0):
                            act.wait_ge(expert_loaded[after], (lap + (1 + (s + 1) // SLOTS)) * 16)
                            settle(act)
                            split_hi(after, FIRST)
                            with act.If(n < 2):
                                split_hi(after, SECOND)
                        later = tile(s == 0, lap * SLOTS + (s + 2))
                        with act.If(n < 2):
                            with act.If(more > 0):
                                split_hi(after, THIRD)
                        with act.If(n > 1):
                            with act.If(more > 0):
                                split_hi(after, SECOND)
                            tile()
                            with act.If(more > 0):
                                split_hi(after, THIRD)
                        with act.If(n > 2):
                            with act.Fori(2, n) as j:
                                tile()
                        act.reg_mov(turns.now, turns.next)
                        act.reg_mov(turns.next, later)
            weigh(turns.t(1))

        @block.vector
        def _(dve):
            ch = Chain(dve, dve_step)

            def normalise(i, src, dst, done):
                settle(dve)
                ch.link(nc.vector.bn_stats(stats[:], src))
                settle(dve)
                ch.link(nc.vector.bn_aggr(mean_var[:], stats[:]))
                nc.vector.tensor_scalar_add(var_eps[:], mean_var[:, 1:2], EPS).then_inc(var_ready, 1)
                dve.wait_ge(rstd_ready, i + 1)
                nc.vector.tensor_scalar(dst[:], src, mean_var[:, 0:1], rstd[:], ALU.subtract, ALU.mult
                                        ).then_inc(done, 1)

            def pair_x(p):
                return xs[:, bass.ds(p, 1), :].rearrange("p a n -> p (a n)")

            def norm_x(p, i):
                if not isinstance(p, int) or p > 0:
                    dve.wait_ge(xt_ready, p)
                normalise(i, pair_x(p), xn, xn_ready)

            def finish_attention(r, i):
                dve.wait_ge(probs_ready, r + 1)
                ch.link(nc.vector.reciprocal(row_inv[:], row_sum[:]))
                dve.wait_ge(rows_used, (r + 1) * GROUPS)
                nc.vector.scalar_tensor_tensor(pair_x(r), b3[:, :], row_inv[:], pair_x(r), ALU.mult, ALU.add
                                               ).then_inc(x1_ready, 1)
                dve.wait_ge(x1_ready, r + 1)
                dve.wait_ge(h_stored, r * 32 + 16)
                dve.wait_ge(ht_ready, r + 1)
                normalise(i, pair_x(r), h, h_ready)

            def score_max(p):
                dve.wait_ge(cols_used, (p + 1) * KD)
                ch.link(nc.vector.reduce_max(row_max[:], scores[:, :, 0:CHUNK], axis=AX.XY))
                dve.wait_ge(c_read, p + 1)
                ch.link(nc.vector.tensor_scalar(max_c[:], row_max[:], c_sb[:], -SCALE, ALU.add, ALU.mult))
                nc.vector.scalar_tensor_tensor(exp_bias[:], c_sb[:], SCALE, max_c[:], ALU.mult, ALU.add
                                               ).then_inc(bias_ready, 1)

            def add_g_bias(p):
                dve.wait_ge(g_ready, 2 * p + 1)
                nc.vector.tensor_tensor(g_t[:], b7[:, :].rearrange("p (k n) -> p k n", k=KD),
                                        fold_cols[:, 0:KD].unsqueeze(2).to_broadcast([P, KD, P]), ALU.add
                                        ).then_inc(gt_ready, 1)

            def read_c(p):
                dve.wait_ge(g_ready, 2 * p + 2)
                dve.wait_ge(bias_ready, p)
                nc.vector.tensor_tensor(c_sb[:], b3[:, 32:33], fold_cols[:, 2 * KD:], ALU.add).then_inc(c_read, 1)

            def route(r):
                dve.wait_ge(gexp_ready, r + 1)
                ch.link(nc.vector.tensor_scalar_add(g_exp1[:], g_exp[:], 1.0))
                ch.link(nc.vector.reciprocal(g_sig[:], g_exp1[:]))
                ch.link(nc.vector.tensor_tensor(g_score[:], g_sig[:], gate_bias[:], ALU.add))
                settle(dve)
                ch.link(nc.vector.max(top[:], g_score[:]))
                settle(dve)
                ch.link(nc.vector.max_index(top_i[:], top[:], g_score[:]))
                ch.mark(nc.vector.reduce_sum(w_sum[:], top[:, 0:TOPK], axis=AX.X))
                ch.link(nc.vector.tensor_copy(top_f[:], top_i[:, 0:TOPK]))
                ch.link(nc.vector.tensor_tensor(onehot[:], iota16.unsqueeze(1).to_broadcast([P, TOPK, EXPERTS]),
                                                top_f[:].unsqueeze(2).to_broadcast([P, TOPK, EXPERTS]),
                                                ALU.is_equal))
                ch.link(nc.vector.reduce_sum(picked[:], onehot[:].rearrange("p k e -> p e k"), axis=AX.X))
                nc.vector.tensor_scalar(mask[:], picked[:], valid, None, ALU.mult).then_inc(mask_ready, 1)
                ch.link(nc.vector.tensor_scalar_add(w_inv[:], w_sum[:], 1e-20))
                ch.link(nc.vector.reciprocal(w_sum[:], w_inv[:]))
                dve.wait_ge(entries_stored, r * (TOPK * 16) + 16)
                nc.vector.tensor_scalar(entry[:, :, 1].bitcast(fp32), top[:, 0:TOPK], w_sum[:], None, ALU.mult)

            def enter(r):
                dve.wait_ge(rank_ready, r + 1)
                nc.vector.tensor_tensor(rank[:], scores[:, 0, 0:EXPERTS], base[:], ALU.add)
                ch.mark(nc.vector.tensor_tensor(base[:], scores[:, 0, EXPERTS:2 * EXPERTS], base[:], ALU.add))
                ch.link(nc.vector.tensor_copy(entry[:, :, 0], token[:].to_broadcast([P, TOPK])))
                ch.link(nc.vector.tensor_tensor(rank_sel[:], onehot[:],
                                                rank[:].unsqueeze(1).to_broadcast([P, TOPK, EXPERTS]), ALU.mult))
                ch.link(nc.vector.reduce_sum(place_f[:], rank_sel[:], axis=AX.X))
                nc.vector.scalar_tensor_tensor(place[:], place_f[:], valid, dump_at[:], ALU.mult, ALU.add
                                               ).then_inc(entries_ready, 1)
                nc.vector.tensor_scalar(dump_at[:], dump_at[:], cst[:, C_STEP:C_STEP + 1], None, ALU.add)
                nc.vector.tensor_scalar_add(token[:], token[:], float(PAIR_TOKENS)).then_inc(rank_read, 1)

            def silu_times_up(uses):
                for i in range(KI):
                    bank = (b6, b7)[i]
                    dve.wait_ge(tanh_ready, uses * KI + (i + 1))
                    ch.link(nc.vector.scalar_tensor_tensor(gated[:, i, :], tanh_half[:, i, :], 1.0, bank[:, 0:P],
                                                           ALU.add, ALU.mult))
                    nc.vector.scalar_tensor_tensor(z[:, i, :], gated[:, i, :], 0.5, bank[:, P:2 * P],
                                                   ALU.mult, ALU.mult).then_inc(z_ready, 1)

            def add_shared(r):
                dve.wait_ge(y_ready, r + 1)
                dve.wait_ge(acc_stored, r * 32 + 16)
                nc.vector.tensor_tensor(acc[:], b3[:, :], pair_x(r), ALU.add).then_inc(acc_ready, 1)

            dve.wait_ge(c_loaded, 16)
            nc.vector.tensor_copy(tri[:], cst[:, C_TRI:C_TRI + P])
            nc.vector.memset(ones[:], 1.0)
            nc.vector.tensor_copy(base[:], region)
            nc.vector.memset(plan_f[0:1, EXPERTS:EXPERTS + 2], 0.0)
            nc.vector.tensor_copy(dump_at[:], cst[:, C_DUMP:C_DUMP + TOPK])
            ch.link(nc.vector.tensor_copy(token[:], cst[:, C_TOK:C_TOK + 1]))
            dve.wait_ge(x_loaded, 64)
            norm_x(0, 0)
            for m, bank in ((2, scores[:, 2, :]), (3, b6[:, :])):
                dve.wait_ge(fold_ready, m + 1)
                nc.vector.tensor_copy(w_fold[:, m, :], bank)
            dve.wait_ge(fold_ready, KD + 1)
            dve.wait_ge(folded_half, 2)
            nc.vector.tensor_copy(fold_cols[:], b7[:, 0:2 * KD + 1]).then_inc(folded, 1)
            dve.wait_ge(folded, 1)
            add_g_bias(0)
            read_c(0)
            norm_x(1, 1)
            score_max(0)
            add_g_bias(1)
            read_c(1)
            dve.wait_ge(sh_loaded, 48)

            def body(p):
                finish_attention(p - 1, p * 2)
                if not isinstance(p, int):
                    norm_x(p + 1, p * 2 + 1)
                score_max(p)
                route(p - 1)
                if not isinstance(p, int):
                    add_g_bias(p + 1)
                    read_c(p + 1)

            start, per = ch.now(), 24
            with dve.Fori(1, PAIRS - 1) as p:
                ch.body(start, p - 1, per)
                body(p)
                silu_times_up(p - 1)
                add_shared(p - 1)
                enter(p - 1)
                assert ch.n == per, ch.n
            last_pair = PAIRS - 1
            ch.base, ch.n = start + (PAIRS - 2) * per, 0
            body(last_pair)
            silu_times_up(last_pair - 1)
            enter(last_pair - 1)
            finish_attention(last_pair, 2 * PAIRS - 1)
            add_shared(last_pair - 1)
            route(last_pair)
            enter(last_pair)

            dve.wait_ge(rank_read, PAIRS)
            ch.link(nc.vector.tensor_tensor(cnt[:], base[0:1, :], region[0:1, :], ALU.subtract))
            ch.link(nc.vector.tensor_tensor(above[:], cnt[:].unsqueeze(2).to_broadcast([1, EXPERTS, TILES_MAX]),
                                            cst[0:1, C_THR:C_ALL].unsqueeze(1).to_broadcast([1, EXPERTS, TILES_MAX]),
                                            ALU.is_gt))
            ch.link(nc.vector.reduce_sum(n_tiles[:], above[:], axis=AX.X))
            ch.link(nc.vector.tensor_scalar_max(n_tiles[0:1, 0:1], n_tiles[0:1, 0:1], 1.0))
            ch.mark(nc.vector.reduce_sum(plan_f[0:1, 2 * EXPERTS + 2:2 * EXPERTS + 3], n_tiles[:], axis=AX.X))
            ch.link(nc.vector.tensor_scalar_min(active[:], n_tiles[:], 1.0))
            ch.link(nc.vector.tensor_tensor_scan(incl[:], cst[0:1, C_ID:C_ID + 1].to_broadcast([1, EXPERTS]),
                                                 active[:], 0.0, ALU.mult, ALU.add))
            ch.link(nc.vector.tensor_tensor(excl[:], incl[:], active[:], ALU.subtract))
            wide = [1, EXPERTS, EXPERTS]
            ch.link(nc.vector.tensor_tensor(turn[:], excl[:].unsqueeze(1).to_broadcast(wide),
                                            iota16[0:1, :].unsqueeze(2).to_broadcast(wide), ALU.is_equal))
            ch.link(nc.vector.tensor_tensor(turn_on[:], turn[:], active[:].unsqueeze(1).to_broadcast(wide), ALU.mult))
            ch.mark(nc.vector.tensor_tensor(turn_n[:], turn_on[:], n_tiles[:].unsqueeze(1).to_broadcast(wide),
                                            ALU.mult))
            ch.link(nc.vector.tensor_tensor(turn_e[:], turn_on[:], iota16[0:1, :].unsqueeze(1).to_broadcast(wide),
                                            ALU.mult))
            ch.mark(nc.vector.tensor_scalar_add(plan_f[0:1, 2 * EXPERTS + 3:],
                                                plan_f[0:1, 2 * EXPERTS + 2:2 * EXPERTS + 3], -float(AHEAD)))
            ch.mark(nc.vector.reduce_sum(plan_f[0:1, 0:EXPERTS], turn_n[:], axis=AX.X))
            ch.link(nc.vector.reduce_sum(plan_f[0:1, EXPERTS + 2:2 * EXPERTS + 2], turn_e[:], axis=AX.X))
            nc.vector.tensor_copy(plan[:], plan_f[:]).then_inc(plan_ready, 1)

            def split_lo(s, blocks, hi_count):
                for i in blocks:
                    src, (hi, lo) = piece(s, i)
                    dve.wait_ge(hi_ready, hi_count + (i + 1))
                    settle(dve)
                    nc.vector.tensor_tensor(lo, src, hi, ALU.subtract).then_inc(lo_ready, 1)

            silu_times_up(last_pair)
            dve.sem_inc(lo_ready, SLOTS * PIECES)
            split_lo(0, FIRST, 0)
            add_shared(last_pair)
            split_lo(0, SECOND, 0)
            split_lo(0, THIRD, 0)

            dve.wait_ge(plan_ready, 1)

            def taken_to_lo(t):
                dve.wait_ge(taken_hi_ready, t + 1)
                settle(dve)
                nc.vector.tensor_tensor(taken_lo[:].rearrange("p k n -> p (k n)"), b4[:, :],
                                        taken_hi[:].rearrange("p k n -> p (k n)"), ALU.subtract
                                        ).then_inc(taken_lo_ready, 1)

            def tile(least, turn=None):
                t = turns.t(least)
                dve.wait_ge(half_ready, t + 1)
                settle(dve)
                nc.vector.scalar_tensor_tensor(gated_rows[:], half_tanh[:], 1.0, b6[:, 0:INNER], ALU.add, ALU.mult
                                               ).then_inc(gated_ready, 1)
                dve.wait_ge(gated_ready, t + 1)
                settle(dve)
                nc.vector.scalar_tensor_tensor(z_rows[:], gated_rows[:], 0.5, b6[:, INNER:], ALU.mult, ALU.mult
                                               ).then_inc(z_rows_ready, 1)
                taken_to_lo(t + 1)
                later = None if turn is None else turns.load(turn)
                dve.wait_ge(zt_hi_ready, t + 1)
                settle(dve)
                nc.vector.tensor_tensor(zt_lo[:].rearrange("p k n -> p (k n)"), b5[:, 0:INNER],
                                        zt_hi[:].rearrange("p k n -> p (k n)"), ALU.subtract
                                        ).then_inc(zt_lo_ready, 1)
                dve.reg_add(turns.tile, turns.tile, 1)
                return later

            taken_to_lo(0)
            turns = Turns(dve, "dve")
            with dve.Fori(0, EXPERTS // SLOTS) as lap:
                for s in range(SLOTS):
                    after = (s + 1) % SLOTS
                    with dve.If(turns.count(turns.now) > 0):
                        hi_count = lap * (SLOTS * PIECES) + (s + 1) * PIECES
                        n, more = turns.count(turns.now), turns.count(turns.next)
                        with dve.If(more > 0):
                            split_lo(after, FIRST, hi_count)
                            with dve.If(n < 2):
                                split_lo(after, SECOND, hi_count)
                        later = tile(0, lap * SLOTS + (s + 2))
                        with dve.If(n < 2):
                            with dve.If(more > 0):
                                split_lo(after, THIRD, hi_count)
                        with dve.If(n > 1):
                            with dve.If(more > 0):
                                split_lo(after, SECOND, hi_count)
                            tile(1)
                            with dve.If(more > 0):
                                split_lo(after, THIRD, hi_count)
                        with dve.If(n > 2):
                            with dve.Fori(2, n) as j:
                                tile(2)
                        dve.reg_mov(turns.now, turns.next)
                        dve.reg_mov(turns.next, later)


def _constants():
    q = np.arange(P)
    c = np.zeros((P, C_ALL), np.float32)
    c[:, C_ID:C_ID + P] = np.eye(P)
    c[:, C_TRI:C_TRI + P] = q[:, None] < q[None, :]
    c[:, C_IOTA:C_IOTA + EXPERTS] = np.arange(EXPERTS)
    c[:, C_REGION:C_REGION + EXPERTS] = np.arange(EXPERTS) * REGION
    real = (q % HALF) < TEXT
    c[:, C_VALID] = real
    for k in range(TOPK):
        c[:, C_DUMP + k] = np.where(real, 0, DUMP + k * P + q)
    c[:, C_STEP] = np.where(real, 0, TOPK * P)
    c[:, C_TOK] = (q // HALF) * TEXT + np.minimum(q % HALF, TEXT - 1)
    c[:, C_THR:C_ALL] = np.arange(TILES_MAX) * P
    lists = np.zeros((P, DUMP // P, 2), np.int32)
    lists[:, :, 0] = TOKENS + np.arange(DUMP // P)[None, :] % P
    return c, lists.reshape(P, -1), np.zeros((HALF - TEXT, PAIRS, DIM), np.float32)


def kernel(**inputs):
    import concourse.bacc as _bacc
    from concourse.bass_utils import run_bass_kernel_spmd as _run

    a = {k: np.asarray(v) for k, v in inputs.items()}
    ctx = a["ctx_4096"]
    ctx_t = ctx.reshape(PAIRS, 2, ROW_TILE, ROW_TILES, KD, P).transpose(0, 4, 5, 1, 3, 2)

    def split(w):
        return w.reshape(KD, P, -1).transpose(1, 0, 2)

    def expert(wg, wu, wd):
        gu = np.stack([wg.swapaxes(-1, -2), wu.swapaxes(-1, -2)], -2)
        lead = gu.shape[:-3]
        gu = np.moveaxis(gu.reshape(*lead, KD, P, 2 * INNER), -3, -2).reshape(*lead, P, -1)
        dn = wd.swapaxes(-1, -2).reshape(*lead, KI, P, DIM)
        dn = np.moveaxis(dn, -3, -2).reshape(*lead, P, -1)
        return np.concatenate([gu, dn], -1)

    c, lists, pad = _constants()
    arrays = {
        "x": a["x"], "ctx": ctx, "ctx_t": ctx_t.reshape(PAIRS, KD, P, 2 * CTX),
        "wq": split(a["L0_xattn_Wq"]), "bq": a["L0_xattn_bq"].reshape(KD, P).T,
        "wk": split(a["L0_xattn_Wk"]), "bk": a["L0_xattn_bk"].reshape(KD, P).T,
        "gate_t": split(a["L0_ffn_gate_w"].T), "gate_b": a["L0_ffn_bias"].reshape(1, EXPERTS),
        "experts": expert(a["L0_ffn_Wg"], a["L0_ffn_Wu"], a["L0_ffn_Wd"]),
        "shared": expert(a["L0_ffn_Sg"], a["L0_ffn_Su"], a["L0_ffn_Sd"]),
        "consts": c, "lists": lists, "pad": pad,
    }
    nc = _bacc.Bacc("TRN2", target_bir_lowering=False, num_devices=1)
    ins, aps = {}, {}
    for name, v in arrays.items():
        v = np.ascontiguousarray(v)
        ins[f"in_{name}"] = v
        aps[name] = nc.dram_tensor(f"in_{name}", v.shape, mybir.dt.from_np(v.dtype), kind="ExternalInput").ap()
    out = nc.dram_tensor("out_0", [TOKENS + P, DIM], mybir.dt.float32, kind="ExternalOutput").ap()
    moe_attention_kernel(nc, aps["x"], aps["ctx"], aps["ctx_t"], aps["wq"], aps["bq"], aps["wk"], aps["bk"],
                         aps["gate_t"], aps["gate_b"], aps["experts"], aps["shared"], aps["consts"],
                         (aps["lists"], aps["pad"]), out)
    r = _run(nc, [ins], core_ids=[0])
    return np.asarray(r.results[0]["out_0"])[:TOKENS].reshape(BATCH, TEXT, DIM)
```
